# Optimizing a Trainium2 kernel written in Bass

```python
import numpy as np
import jax
import jax.numpy as jnp

def _softmax(x, axis=-1):
    return jax.nn.softmax(x, axis=axis)

def _gelu(x):
    return jax.nn.gelu(x, approximate=True)

def _silu(x):
    return jax.nn.silu(x)

def _sigmoid(x):
    return jax.nn.sigmoid(x)

def _layernorm(x, axis=-1, eps=1e-05):
    m = jnp.mean(x, axis=axis, keepdims=True)
    v = jnp.var(x, axis=axis, keepdims=True)
    return (x - m) / jnp.sqrt(v + eps)

def _scatter_add(tgt, idx, src, axis=0):
    return tgt.at[idx].add(src)

def _segment_sum(src, seg, n):
    return jax.ops.segment_sum(src, seg, n)
kernel_name = 'mk_adj_resnorm_d4_adj_r2_5a3117'

def setup_inputs(seed: int=0):
    np.random.seed(seed)
    _w = jnp.asarray

    def _rec_inputs():
        import jax
        import jax.numpy as jnp
        _gk = jax.random.key(seed)
        x = -0.001547 + 1.001 * jax.random.normal(jax.random.fold_in(_gk, 1), (8192, 64), jnp.float32)
        _a = jax.random.bernoulli(jax.random.fold_in(_gk, 2), 0.000244141, (8192, 8192))
        _a = jnp.logical_or(_a, jnp.swapaxes(_a, -1, -2))
        _a = jnp.logical_or(_a, jnp.eye(8192, dtype=bool))
        adj = _a.astype(jnp.int32)
        return (x, adj)
    x, adj = _rec_inputs()

    def _L0_gnn_setup():
        import jax, jax.numpy as jnp
        import numpy as np
        N = 2048
        C = 64
        GDEP = 2
        HID = 32
        ALPHA = 0.2
        NEG_INF = jnp.float32(-9000000000000000.0)

        def _gat_layer(h, adj_mask, W_l, lw, lb, a):
            Wh = h @ W_l
            L1, L2 = (lw[:C], lw[C:])
            u = Wh @ L1 @ a
            v = Wh @ L2 @ a
            c = lb @ a
            e = jax.nn.leaky_relu(u + v.T + c, negative_slope=ALPHA)
            scores = jnp.where(adj_mask, e, NEG_INF)
            att = jax.nn.softmax(scores, axis=1)
            return jax.nn.elu(att @ Wh)
        key = jax.random.key(seed)
        ks = jax.random.split(key, 8)
        x = jax.random.normal(ks[0], (N, C), jnp.float32)
        adj = jax.random.randint(ks[1], (N, N), 0, 2, jnp.int32)
        W = jax.random.normal(ks[2], (GDEP, C, C), jnp.float32) / np.sqrt(C)
        lin_w = jax.random.normal(ks[3], (GDEP, 2 * C, HID), jnp.float32) / np.sqrt(2 * C)
        lin_b = jnp.zeros((GDEP, HID), jnp.float32)
        attn = jax.random.normal(ks[4], (GDEP, HID, 1), jnp.float32) / np.sqrt(HID)
        mlp_w = jax.random.normal(ks[5], ((GDEP + 1) * C, C), jnp.float32) / np.sqrt((GDEP + 1) * C)
        mlp_b = jnp.zeros((C,), jnp.float32)
        return dict(x=x, adj=adj, W=W, lin_w=lin_w, lin_b=lin_b, attn=attn, mlp_w=mlp_w, mlp_b=mlp_b)
    _L0_gnn_all = _L0_gnn_setup()
    _L0_gnn_in = {k: v for k, v in _L0_gnn_all.items() if k in ('W', 'lin_w', 'lin_b', 'attn', 'mlp_w', 'mlp_b')}
    del _L0_gnn_all

    def _L1_gnn_setup():
        import jax, jax.numpy as jnp
        import numpy as np
        N = 10000
        F = 64
        O = 64
        key = jax.random.key(seed)
        k1, k2, k3 = jax.random.split(key, 3)
        x = jax.random.normal(k1, (N, F), dtype=jnp.float32)
        adj = jax.random.randint(k2, (N, N), 0, 2, dtype=jnp.int32)
        stdv = float(np.sqrt(6.0 / (2 * F + O)))
        weight = jax.random.uniform(k3, (2 * F, O), dtype=jnp.float32, minval=-stdv, maxval=stdv)
        bias = jnp.zeros((O,), dtype=jnp.float32)
        return {'x': x, 'adj': adj, 'weight': weight, 'bias': bias}
    _L1_gnn_all = _L1_gnn_setup()
    _L1_gnn_in = {k: v for k, v in _L1_gnn_all.items() if k in ('weight', 'bias')}
    del _L1_gnn_all

    def _L2_gnn_setup():
        import jax, jax.numpy as jnp
        import numpy as np
        N = 6144
        IN_C = 64
        OUT_C = 64
        NEG_INF = -1000000000.0
        key = jax.random.key(seed)
        k1, k2, k3, k4 = jax.random.split(key, 4)
        x = jax.random.normal(k1, (N, IN_C), dtype=jnp.float32)
        edge_index = jax.random.randint(k2, (N, N), 0, 2, dtype=jnp.int32)
        weight_w = jax.random.normal(k3, (IN_C, OUT_C), dtype=jnp.float32) * (1.0 / np.sqrt(IN_C))
        weight_a = jax.random.normal(k4, (2 * OUT_C, 1), dtype=jnp.float32) * (1.0 / np.sqrt(OUT_C))
        bias = jnp.zeros((OUT_C,), dtype=jnp.float32)
        return {'x': x, 'edge_index': edge_index, 'weight_w': weight_w, 'weight_a': weight_a, 'bias': bias}
    _L2_gnn_all = _L2_gnn_setup()
    _L2_gnn_in = {k: v for k, v in _L2_gnn_all.items() if k in ('weight_w', 'weight_a', 'bias')}
    del _L2_gnn_all

    def _L3_gnn_setup():
        import jax, jax.numpy as jnp
        import numpy as np
        ALPHA = 0.2
        NEG_INF = -9000000000000000.0
        key = jax.random.key(seed)
        k1, k2, k3, k4 = jax.random.split(key, 4)
        N, F_IN, F_OUT = (512, 64, 64)
        h = jax.random.normal(k1, (N, F_IN), dtype=jnp.float32)
        adj = jax.random.randint(k2, (N, N), 0, 2, dtype=jnp.int32)
        lim_W = 1.414 * np.sqrt(6.0 / (F_IN + F_OUT))
        W = jax.random.uniform(k3, (F_IN, F_OUT), minval=-lim_W, maxval=lim_W, dtype=jnp.float32)
        lim_a = 1.414 * np.sqrt(6.0 / (2 * F_OUT + 1))
        a = jax.random.uniform(k4, (2 * F_OUT, 1), minval=-lim_a, maxval=lim_a, dtype=jnp.float32)
        return {'h': h, 'adj': adj, 'W': W, 'a': a}
    _L3_gnn_all = _L3_gnn_setup()
    _L3_gnn_in = {k: v for k, v in _L3_gnn_all.items() if k in ('W', 'a')}
    del _L3_gnn_all
    return {'x': x, 'adj': adj, 'L0_gnn_W': _L0_gnn_in['W'], 'L0_gnn_lin_w': _L0_gnn_in['lin_w'], 'L0_gnn_lin_b': _L0_gnn_in['lin_b'], 'L0_gnn_attn': _L0_gnn_in['attn'], 'L0_gnn_mlp_w': _L0_gnn_in['mlp_w'], 'L0_gnn_mlp_b': _L0_gnn_in['mlp_b'], 'L1_gnn_weight': _L1_gnn_in['weight'], 'L1_gnn_bias': _L1_gnn_in['bias'], 'L2_gnn_weight_w': _L2_gnn_in['weight_w'], 'L2_gnn_weight_a': _L2_gnn_in['weight_a'], 'L2_gnn_bias': _L2_gnn_in['bias'], 'L3_gnn_W': _L3_gnn_in['W'], 'L3_gnn_a': _L3_gnn_in['a']}

def reference(x, adj, L0_gnn_W, L0_gnn_lin_w, L0_gnn_lin_b, L0_gnn_attn, L0_gnn_mlp_w, L0_gnn_mlp_b, L1_gnn_weight, L1_gnn_bias, L2_gnn_weight_w, L2_gnn_weight_a, L2_gnn_bias, L3_gnn_W, L3_gnn_a):
    import jax
    import jax.numpy as jnp

    def _L0_gnn_ref(x, adj, W, lin_w, lin_b, attn, mlp_w, mlp_b):
        import jax, jax.numpy as jnp
        import numpy as np
        N = 2048
        C = 64
        GDEP = 2
        HID = 32
        ALPHA = 0.2
        NEG_INF = jnp.float32(-9000000000000000.0)

        def _gat_layer(h, adj_mask, W_l, lw, lb, a):
            Wh = h @ W_l
            L1, L2 = (lw[:C], lw[C:])
            u = Wh @ L1 @ a
            v = Wh @ L2 @ a
            c = lb @ a
            e = jax.nn.leaky_relu(u + v.T + c, negative_slope=ALPHA)
            scores = jnp.where(adj_mask, e, NEG_INF)
            att = jax.nn.softmax(scores, axis=1)
            return jax.nn.elu(att @ Wh)
        mask = adj > 0
        h = x
        outs = [h]
        for i in range(GDEP):
            h = ALPHA * x + (1.0 - ALPHA) * _gat_layer(h, mask, W[i], lin_w[i], lin_b[i], attn[i])
            outs.append(h)
        ho = jnp.concatenate(outs, axis=-1)
        return ho @ mlp_w + mlp_b

    def _L1_gnn_ref(x, adj, weight, bias):
        import jax, jax.numpy as jnp
        import numpy as np
        N = 10000
        F = 64
        O = 64
        a = (adj == 1).astype(x.dtype)
        deg = jnp.sum(a, axis=1, keepdims=True)
        x1 = a @ x / deg
        n_x = jnp.concatenate([x1, x], axis=1)
        return n_x @ weight + bias

    def _L2_gnn_ref(x, edge_index, weight_w, weight_a, bias):
        import jax, jax.numpy as jnp
        import numpy as np
        N = 6144
        IN_C = 64
        OUT_C = 64
        NEG_INF = -1000000000.0
        wh = x @ weight_w
        a_src = weight_a[:OUT_C, 0]
        a_dst = weight_a[OUT_C:, 0]
        e = (wh @ a_src)[:, None] + (wh @ a_dst)[None, :]
        e = jax.nn.leaky_relu(e, negative_slope=0.01)
        scores = jnp.where(edge_index > 0, e, NEG_INF)
        attention = jax.nn.softmax(scores, axis=1)
        out = attention @ wh
        return out + bias

    def _L3_gnn_ref(h, adj, W, a):
        import jax, jax.numpy as jnp
        import numpy as np
        ALPHA = 0.2
        NEG_INF = -9000000000000000.0
        F_OUT = W.shape[1]
        Wh = h @ W
        a1, a2 = (a[:F_OUT, 0], a[F_OUT:, 0])
        e = (Wh @ a1)[:, None] + (Wh @ a2)[None, :]
        e = jax.nn.leaky_relu(e, negative_slope=ALPHA)
        scores = jnp.where(adj > 0, e, jnp.float32(NEG_INF))
        attention = jax.nn.softmax(scores, axis=1)
        h_prime = attention @ Wh
        return jax.nn.elu(h_prime)
    x = _layernorm(x + _L0_gnn_ref(x, adj, L0_gnn_W, L0_gnn_lin_w, L0_gnn_lin_b, L0_gnn_attn, L0_gnn_mlp_w, L0_gnn_mlp_b), axis=-1)
    x = _layernorm(x + _L1_gnn_ref(x, adj, L1_gnn_weight, L1_gnn_bias), axis=-1)
    x = _layernorm(x + _L2_gnn_ref(x, adj, L2_gnn_weight_w, L2_gnn_weight_a, L2_gnn_bias), axis=-1)
    x = _layernorm(x + _L3_gnn_ref(x, adj, L3_gnn_W, L3_gnn_a), axis=-1)
    return x

_drawn_inputs = setup_inputs


def setup_inputs(seed=0):
    import zlib

    import numpy as np

    out = dict(_drawn_inputs(seed))
    spreads = {'L0_gnn_lin_b': (0.0, 0.8),
     'L0_gnn_mlp_b': (0.0, 0.1),
     'L1_gnn_bias': (0.0, 0.1),
     'L2_gnn_bias': (0.0, 0.1)}
    factors = {}
    for name, (base, spread) in spreads.items():
        noise = np.random.default_rng([zlib.crc32(name.encode()), seed]).standard_normal(out[name].shape)
        drawn = base * np.exp(spread * noise) if base else spread * noise
        out[name] = jnp.asarray(drawn.astype(out[name].dtype))
    for name, factor in factors.items():
        out[name] = (out[name] * factor).astype(out[name].dtype)
    return out
```

```python
from contextlib import ExitStack

import numpy as np

import concourse.bass as bass
from concourse import mybir

F32 = mybir.dt.float32
BF16 = mybir.dt.bfloat16
I32 = mybir.dt.int32
ALU = mybir.AluOpType
ACT = mybir.ActivationFunctionType
AX = mybir.AxisListType.X

P = 128
N = 8192
C = 64
NT = N // P
TC = C + 2
RC = TC + C
UT = 4
NU = NT // UT
GT = 8
NG = NT // GT
HALF = N // 2
TB = 4
NB = NT // TB
NEG = 9.0e15
EPS = 1e-5
HID = 32
L0_MIX = 0.2

SLOPE = [0.2, 0.2, None, 0.01, 0.2]
NL = len(SLOPE)

MLP2 = NL * RC
WT = MLP2 + C
A2 = WT + 4 * (C + 1)
LT = A2 + 4
AV = LT + 2 * 2 * C
LB = AV + 2
BLOB = LB + 2 * (C + 1)
WT_OF = {0: 0, 1: 1, 3: 2, 4: 3}


class Count:

    def __init__(self, sem):
        self.sem, self.base, self.turn, self.per, self.k = sem, 0, 0, 0, 0

    def loop(self, turn, per):
        self.base, self.turn, self.per, self.k = self.base + self.k, turn, per, 0

    def end(self, turns):
        assert self.k == self.per, (self.k, self.per)
        self.base, self.turn, self.per, self.k = self.base + turns * self.per, 0, 0, 0

    def at(self):
        return self.turn * self.per + (self.base + self.k) if self.per else self.base + self.k


def build(nc, x_in, adj_in, blob_in, out):
    adj_t = adj_in.rearrange("(t p) j -> t p j", p=P)
    with ExitStack() as ctx:
        def sb(name, shape, dt):
            return ctx.enter_context(nc.sbuf_tensor(name, shape, dt))

        def sem(name):
            return ctx.enter_context(nc.semaphore(name))

        x = sb("nodes", [P, NT, C], F32)
        res = sb("res", [P, NT, C], F32)
        hid = sb("hid", [P, NT, C], F32)
        tab = sb("tab", [P, NT, TC], F32)
        own = sb("own", [P, NT], F32)
        w = sb("w", [P, BLOB], F32)
        ident = sb("ident", [P, P], F32)
        ones = sb("ones", [P, P], F32)
        xt = sb("xt", [C + 1, 2, UT * P], F32)
        a2 = sb("a2", [C, 2, 2], F32)
        stat = sb("stat", [P, NT], F32)
        mean = sb("mean", [P, NT], F32)
        vb = sb("vb", [P, N], F32)
        adjb = sb("adjb", [P, 2, HALF], I32)
        s = sb("s", [P, 2, N], F32)
        pt = sb("pt", [P, 2, TB * P], F32)
        stage = pt[:, :, 0:UT * C].rearrange("p b (k c) -> p b k c", c=C)
        nmax = sb("nmax", [P, 2], F32)
        rden = sb("rden", [P, 2], F32)
        ps = ctx.enter_context(nc.psum_tensor("ps", [P, 8, 512], F32))
        big = s[:, :, :].rearrange("p a (t c) -> p (a t) c", c=C)
        sqs = big[:, 0:NT, :]

        x_loaded = sem("x_loaded")
        w_loaded = sem("w_loaded")
        const_made = sem("const_made")
        vec_const = sem("vec_const")
        w_mm = sem("w_mm")
        w_cp = sem("w_cp")
        staged = sem("staged")
        t_turned = sem("t_turned")
        xt_copied = sem("xt_copied")
        proj_done = sem("proj_done")
        proj_used = sem("proj_used")
        nodes_ready = sem("nodes_ready")
        diag_made = sem("diag_made")
        vb_summed = sem("vb_summed")
        vb_ready = sem("vb_ready")
        adj_loaded = [sem("adj_loaded0"), sem("adj_loaded1")]
        adj_used = sem("adj_used")
        z_ready = sem("z_ready")
        max_ready = sem("max_ready")
        p_ready = sem("p_ready")
        m_ready = sem("m_ready")
        p_turned = sem("p_turned")
        pt_copied = sem("pt_copied")
        pt_used = sem("pt_used")
        agg_used = sem("agg_used")
        vec_step = sem("vec_step")
        elu_in = sem("elu_in")
        elu_exp = sem("elu_exp")
        var_ready = sem("var_ready")
        std_ready = sem("std_ready")
        out_stored = sem("out_stored")
        block = ctx.enter_context(nc.Block())

        GATS = [l for l in range(NL) if SLOPE[l] is not None]
        STAGES = [0, 1, None, 2, 3, 4]

        def gats_before(l):
            return sum(k < l for k in GATS)

        def stages_before(l):
            return STAGES.index(l)

        @block.sync
        def _(sp):
            sp.dma_start(x[:, :, :], x_in.rearrange("(t p) c -> p t c", p=P)).then_inc(x_loaded, 16)
            sp.dma_start(w[0:C + 1, :], blob_in).then_inc(w_loaded, 16)
            for l in range(NL):
                def load(t):
                    for h in range(2):
                        if not (l == 0 and isinstance(t, int) and t == 0):
                            sp.wait_ge(adj_used, (t + (l * NT - 1)) * 2 + h + 1)
                        sp.dma_start(adjb[:, h, :], adj_t[bass.ds(t, 1), :, h * HALF:(h + 1) * HALF].rearrange(
                            "a p j -> p (a j)")).then_inc(adj_loaded[h], 16)
                load(0)
                with sp.Fori(1, NT) as t:
                    load(t)
            sp.wait_ge(nodes_ready, NL + 1)
            sp.dma_start(out.rearrange("(t p) c -> p t c", p=P), x[:, :, :]).then_inc(out_stored, 16)
            sp.wait_ge(out_stored, 16)

        @block.gpsimd
        def _(pool):
            pool.memset(ident[:, :], 0.0).then_inc(const_made, 1)
            pool.memset(ones[:, :], 1.0).then_inc(const_made, 1)
            pool.memset(tab[:, :, C + 1:C + 2], 1.0).then_inc(const_made, 1)
            pool.wait_ge(const_made, 3)
            pool.memset(xt[C:C + 1, :, :], 1.0).then_inc(const_made, 1)
            pool.wait_ge(const_made, 4)
            pool.affine_select(out=ident[:, :], in_=ident[:, :], compare_op=ALU.not_equal, fill=1.0,
                               base=0, pattern=[[-1, P]], channel_multiplier=1).then_inc(const_made, 1)

        @block.tensor
        def _(pe):
            pe.wait_ge(w_loaded, 16)
            pe.wait_ge(const_made, 5)
            for l in range(2):
                for k in range(2):
                    mm = pe.matmul(ps[0:C, 0, 2 * l + k:2 * l + k + 1], w[0:HID, LT + (2 * l + k) * C:LT + (2 * l + k + 1) * C],
                                   w[0:HID, AV + l:AV + l + 1], start=True, stop=True)
            mm.then_inc(w_mm, 1)
            pe.wait_ge(w_cp, 1)
            for l in GATS:
                o = ps[0:C + 1, 1 + WT_OF[l], 0:2]
                rhs = a2[:, l, :] if l < 2 else w[0:C, A2 + 2 * (l - 3):A2 + 2 * (l - 2)]
                lhs = w[0:C, WT + WT_OF[l] * (C + 1):WT + (WT_OF[l] + 1) * (C + 1)]
                mm = pe.matmul(o, lhs, rhs, start=True, stop=(l >= 2))
                if l < 2:
                    mm = pe.matmul(ps[0:C + 1, 1 + WT_OF[l], 1:2], w[0:HID, LB + l * (C + 1):LB + (l + 1) * (C + 1)],
                                   w[0:HID, AV + l:AV + l + 1], start=False, stop=True)
            mm.then_inc(w_mm, 1)
            pe.wait_ge(x_loaded, 16)
            pe.wait_ge(w_cp, 2)

            def turn(base, q, b, first):
                if not first:
                    pe.wait_ge(xt_copied, q + (base - 1))
                pe.wait_ge(staged, q + (base + 1))
                for k in range(UT):
                    mm = pe.matmul(ps[0:C, b, k * P:(k + 1) * P], stage[:, b, k, :], ident[:, :], start=True, stop=True)
                mm.then_inc(t_turned, 1)

            def product(n, base, q, b, first):
                pe.wait_ge(xt_copied, q + (base + 1))
                if not first:
                    pe.wait_ge(proj_used, q + (base - 1))
                l = STAGES[n]
                for k in range(UT):
                    o = ps[:, 2 + 2 * b + k // 2, :]
                    lhs = xt[:, b, k * P:(k + 1) * P]
                    if l is None:
                        mm = pe.matmul(o[:, (k % 2) * RC:(k % 2) * RC + C], lhs, w[0:C + 1, MLP2:MLP2 + C],
                                       start=True, stop=True)
                    else:
                        mm = pe.matmul(o[:, (k % 2) * RC:(k % 2 + 1) * RC], lhs, w[0:C + 1, l * RC:(l + 1) * RC],
                                       start=True, stop=True)
                mm.then_inc(proj_done, 1)

            def project(n):
                base = n * NU
                turn(base, 0, 0, n == 0)
                turn(base, 1, 1, n == 0)
                product(n, base, 0, 0, n == 0)
                product(n, base, 1, 1, n == 0)
                with pe.Fori(1, NU // 2) as i:
                    for b in range(2):
                        turn(base, 2 * i + b, b, False)
                    for b in range(2):
                        product(n, base, 2 * i + b, b, False)

            def spread(l):
                base = gats_before(l) * NU
                pe.wait_ge(proj_used, (stages_before(l) + 1) * NU)

                def unit(q, b, first):
                    pe.wait_ge(diag_made, q + (base + 1))
                    if not first:
                        pe.wait_ge(vb_ready, q + (base - 1))
                    pe.matmul(ps[:, b, :], ones[:, :], pt[:, b, :], start=True, stop=True).then_inc(vb_summed, 1)
                unit(0, 0, l == 0)
                unit(1, 1, l == 0)
                with pe.Fori(1, NU // 2) as i:
                    for b in range(2):
                        unit(2 * i + b, b, False)
                pe.wait_ge(vb_ready, base + NU)

            def aggregate(l):
                if SLOPE[l] is not None:
                    spread(l)
                else:
                    pe.wait_ge(proj_used, (stages_before(l) + 1) * NU)

                def tile(t, b, first):
                    if SLOPE[l] is None:
                        pe.wait_ge(m_ready, t + 1)
                    else:
                        pe.wait_ge(p_ready, t + (gats_before(l) * NT + 1))
                    tb = t * NB + l * NT * NB

                    def turned(g):
                        if not (first and g < 2):
                            pe.wait_ge(pt_copied, tb + (g - 1))
                        for k in range(TB):
                            j = g * TB + k
                            mm = pe.transpose(ps[:, g % 2, k * P:(k + 1) * P], s[:, b, j * P:(j + 1) * P], ident[:, :])
                        mm.then_inc(p_turned, 1)

                    def summed(g):
                        pe.wait_ge(pt_copied, tb + (g + 1))
                        for k in range(TB):
                            j = g * TB + k
                            mm = pe.matmul(ps[:, 2 + b, 0:TC], pt[:, g % 2, k * P:(k + 1) * P], tab[:, j, :],
                                           start=(j == 0), stop=(j == NT - 1))
                        mm.then_inc(pt_used, 1)

                    turned(0)
                    if not (l == 0 and isinstance(t, int) and t < 2):
                        pe.wait_ge(agg_used, t + (l * NT - 1))
                    for g in range(NB):
                        if g + 1 < NB:
                            turned(g + 1)
                        summed(g)

                tile(0, 0, l == 0)
                tile(1, 1, False)
                with pe.Fori(1, NT // 2) as i:
                    for b in range(2):
                        tile(2 * i + b, b, False)

            for n, l in enumerate(STAGES):
                project(n)
                if l is not None:
                    aggregate(l)

        @block.scalar
        def _(act):
            def project(n):
                base = n * NU

                src = hid if n in (1, 2) else x

                def put(q, b, first):
                    if not first:
                        act.wait_ge(t_turned, q + (base - 1))
                    act.activation(stage[:, b, :, :], src[:, bass.ds(q * UT, UT), :], ACT.Copy).then_inc(staged, 1)

                def unit(q, b, first):
                    act.wait_ge(t_turned, q + (base + 1))
                    if not first:
                        act.wait_ge(proj_done, q + (base - 1))
                    act.activation(xt[0:C, b, :], ps[0:C, b, :], ACT.Copy).then_inc(xt_copied, 1)

                if n > 0:
                    act.wait_ge(nodes_ready, n)
                else:
                    act.wait_ge(x_loaded, 16)
                put(0, 0, n == 0)
                put(1, 1, n == 0)
                unit(0, 0, n == 0)
                put(2, 0, False)
                unit(1, 1, n == 0)
                with act.Fori(1, NU // 2 - 1) as i:
                    for b in range(2):
                        put(2 * i + (b + 1), 1 - b, False)
                        unit(2 * i + b, b, False)
                put(NU - 1, 1, False)
                unit(NU - 2, 0, False)
                unit(NU - 1, 1, False)

            def aggregate(l):
                gat = SLOPE[l] is not None
                gb = gats_before(l) * NT
                if gat:
                    base = gats_before(l) * NU
                    with act.Fori(0, NU // 2) as i:
                        for b in range(2):
                            act.wait_ge(vb_summed, 2 * i + (base + b + 1))
                            act.activation(vb[:, bass.ds((2 * i + b) * UT * P, UT * P)], ps[:, b, :], ACT.Copy).then_inc(vb_ready, 1)
                    act.wait_ge(vb_ready, base + NU)

                def scores(t, b, first):
                    if not first:
                        act.wait_ge(pt_used, (t + (l * NT - 1)) * NB)
                    act.activation(s[:, b, :], vb[:, :], ACT.Identity, bias=own[:, bass.ds(t, 1)]).then_inc(z_ready, 1)

                def tile(t, b, first):
                    if gat:
                        act.wait_ge(max_ready, t + (gb + 1))
                        act.activation(s[:, b, :], s[:, b, :], ACT.Exp, bias=nmax[:, b:b + 1]).then_inc(p_ready, 1)
                    tb = t * NB + l * NT * NB
                    for g in range(NB):
                        act.wait_ge(p_turned, tb + (g + 1))
                        if not (first and g < 2):
                            act.wait_ge(pt_used, tb + (g - 1))
                        act.activation(pt[:, g % 2, :], ps[:, g % 2, :], ACT.Copy).then_inc(pt_copied, 1)

                if gat:
                    scores(0, 0, True)
                    scores(1, 1, True)
                tile(0, 0, l == 0)
                if gat:
                    scores(2, 0, False)
                tile(1, 1, False)
                with act.Fori(1, NT // 2 - 1) as i:
                    for b in range(2):
                        if gat:
                            scores(2 * i + (b + 1), 1 - b, False)
                        tile(2 * i + b, b, False)
                if gat:
                    scores(NT - 1, 1, False)
                tile(NT - 2, 0, False)
                tile(NT - 1, 1, False)

            elus = 0
            lns = 0
            for n, l in enumerate(STAGES):
                project(n)
                if l is not None:
                    aggregate(l)
                if l in (0, 1, 4):
                    elus += 1
                    act.wait_ge(elu_in, elus)
                    act.activation(big[:, 0:NT, :], big[:, 0:NT, :], ACT.Exp).then_inc(elu_exp, 1)
                if l not in (0, 1):
                    lns += 1
                    act.wait_ge(var_ready, lns)
                    act.activation(stat[:, :], stat[:, :], ACT.Sqrt).then_inc(std_ready, 1)

        @block.vector
        def _(dve):
            step = Count(vec_step)

            def link(ins):
                ins.then_inc(vec_step, 1)
                step.k += 1
                dve.wait_ge(vec_step, step.at())

            dve.wait_ge(w_loaded, 16)
            dve.wait_ge(w_mm, 1)
            dve.tensor_copy(a2[:, :, :], ps[0:C, 0, 0:4].rearrange("p (l k) -> p l k", l=2)).then_inc(w_cp, 1)
            dve.wait_ge(w_mm, 2)
            for l in GATS:
                cp = dve.tensor_copy(w[0:C + 1, l * RC + C:l * RC + TC], ps[0:C + 1, 1 + WT_OF[l], 0:2])
            cp.then_inc(w_cp, 1)
            dve.wait_ge(x_loaded, 16)
            dve.wait_ge(const_made, 5)

            def project(n):
                l = STAGES[n]
                base = n * NU
                with dve.Fori(0, NU // 2) as i:
                    for b in range(2):
                        q = 2 * i + b
                        dve.wait_ge(proj_done, q + (base + 1))
                        r = res[:, bass.ds(q * UT, UT), :].rearrange("p (a k) c -> p a k c", k=2)
                        xs = x[:, bass.ds(q * UT, UT), :].rearrange("p (a k) c -> p a k c", k=2)
                        both = ps[:, 2 + 2 * b:4 + 2 * b, 0:2 * RC].rearrange("p a (k c) -> p a k c", k=2)
                        if l is None:
                            dve.tensor_tensor(r, both[:, :, :, 0:C], r, ALU.add).then_inc(proj_used, 1)
                            continue
                        dve.tensor_copy(tab[:, bass.ds(q * UT, UT), 0:C + 1].rearrange("p (a k) c -> p a k c", k=2),
                                        both[:, :, :, 0:C + 1])
                        dve.tensor_copy(own[:, bass.ds(q * UT, UT)].rearrange("p (a k) -> p a k", k=2),
                                        both[:, :, :, C + 1])
                        dve.tensor_tensor(r, both[:, :, :, TC:RC], r if n == 1 else xs, ALU.add).then_inc(proj_used, 1)
                dve.wait_ge(proj_used, base + NU)

            def aggregate(l):
                gat = SLOPE[l] is not None
                if gat:
                    base = gats_before(l) * NU

                    def diagonals(q, b, first):
                        if not first:
                            dve.wait_ge(vb_summed, q + (base - 1))
                        for k in range(UT):
                            d = dve.tensor_scalar(pt[:, b, k * P:(k + 1) * P], ident[:, :],
                                                  tab[:, bass.ds(q * UT + k, 1), C:C + 1].rearrange(
                                                      "p a c -> p (a c)"), None, ALU.mult)
                        d.then_inc(diag_made, 1)
                    diagonals(0, 0, l == 0)
                    diagonals(1, 1, l == 0)
                    with dve.Fori(1, NU // 2) as i:
                        for b in range(2):
                            diagonals(2 * i + b, b, False)

                def edges(t, b):
                    if gat:
                        dve.wait_ge(z_ready, t + (gats_before(l) * NT + 1))
                        link(dve.scalar_tensor_tensor(out=s[:, b, :], in0=s[:, b, :], scalar=SLOPE[l], in1=s[:, b, :],
                                                      op0=ALU.mult, op1=ALU.max))
                    elif not (isinstance(t, int) and t < 2):
                        dve.wait_ge(pt_used, (t + (l * NT - 1)) * NB)
                    for h in range(2):
                        dve.wait_ge(adj_loaded[h], t * 16 + (l * NT + 1) * 16)
                        sh = s[:, b, h * HALF:(h + 1) * HALF]
                        if gat:
                            m = adjb[:, h, :].bitcast(F32)
                            link(dve.tensor_scalar(m, adjb[:, h, :], 0, NEG, ALU.is_gt, ALU.mult))
                            dve.scalar_tensor_tensor(out=sh, in0=m, scalar=-NEG, in1=sh,
                                                     op0=ALU.add, op1=ALU.add).then_inc(adj_used, 1)
                        else:
                            dve.tensor_scalar(sh, adjb[:, h, :], 1, None, ALU.is_equal).then_inc(adj_used, 1)
                    dve.wait_ge(adj_used, t * 2 + (l * NT * 2 + 2))
                    if gat:
                        dve.tensor_reduce(nmax[:, b:b + 1], s[:, b, :], AX, ALU.max, negate=True).then_inc(max_ready, 1)
                    else:
                        dve.tensor_copy(nmax[:, b:b + 1], ones[:, 0:1]).then_inc(m_ready, 1)

                def divided(t, b):
                    dve.wait_ge(pt_used, (t + (l * NT + 1)) * NB)
                    link(dve.reciprocal(rden[:, b:b + 1], ps[:, 2 + b, C + 1:TC]))
                    dve.tensor_scalar(hid[:, bass.ds(t, 1), :].rearrange("p a c -> p (a c)"), ps[:, 2 + b, 0:C],
                                      rden[:, b:b + 1], None, ALU.mult).then_inc(agg_used, 1)

                edges(0, 0)
                edges(1, 1)
                divided(0, 0)
                with dve.Fori(1, NT // 2) as i:
                    step.loop(i - 1, 2 * (4 if gat else 1))
                    for b in range(2):
                        edges(2 * i + b, b)
                        divided(2 * i + (b - 1), 1 - b)
                    step.end(NT // 2 - 1)
                divided(NT - 1, 1)
                dve.wait_ge(agg_used, (l + 1) * NT)

            def elu(k):
                e = big[:, 0:NT, :]
                dve.tensor_scalar(e, hid[:, :, :], 0.0, None, ALU.min).then_inc(elu_in, 1)
                dve.wait_ge(elu_exp, k)
                link(dve.scalar_tensor_tensor(out=hid[:, :, :], in0=hid[:, :, :], scalar=0.0, in1=e,
                                              op0=ALU.max, op1=ALU.add))

            def mixed():
                link(dve.tensor_scalar(big[:, 0:NT, :], x[:, :, :], L0_MIX, L0_MIX - 1.0, ALU.mult, ALU.add))
                dve.scalar_tensor_tensor(out=hid[:, :, :], in0=hid[:, :, :], scalar=1.0 - L0_MIX, in1=big[:, 0:NT, :],
                                         op0=ALU.mult, op1=ALU.add).then_inc(nodes_ready, 1)

            def normed(k):
                bc = [P, NT, C]
                link(dve.tensor_reduce(mean[:, :], res[:, :, :], AX, ALU.add))
                link(dve.tensor_scalar(mean[:, :], mean[:, :], -1.0 / C, None, ALU.mult))
                link(dve.tensor_tensor(res[:, :, :], res[:, :, :], mean[:, :].unsqueeze(2).to_broadcast(bc), ALU.add))
                link(dve.tensor_tensor(sqs, res[:, :, :], res[:, :, :], ALU.mult))
                link(dve.tensor_reduce(stat[:, :], sqs, AX, ALU.add))
                dve.tensor_scalar(stat[:, :], stat[:, :], 1.0 / C, EPS, ALU.mult, ALU.add).then_inc(var_ready, 1)
                dve.wait_ge(std_ready, k)
                link(dve.reciprocal(mean[:, :], stat[:, :]))
                dve.tensor_tensor(x[:, :, :], res[:, :, :], mean[:, :].unsqueeze(2).to_broadcast(bc),
                                  ALU.mult).then_inc(nodes_ready, 1)

            project(0)
            aggregate(0)
            elu(1)
            mixed()
            project(1)
            aggregate(1)
            elu(2)
            mixed()
            project(2)
            normed(1)
            for l in (2, 3, 4):
                dve.wait_ge(nodes_ready, l + 1)
                project(l + 1)
                aggregate(l)
                if l == 4:
                    elu(3)
                    link(dve.scalar_tensor_tensor(out=res[:, :, :], in0=hid[:, :, :], scalar=-1.0, in1=res[:, :, :],
                                                  op0=ALU.add, op1=ALU.add))
                else:
                    link(dve.tensor_tensor(res[:, :, :], hid[:, :, :], res[:, :, :], ALU.add))
                normed(l)


def packed(i):
    f = {k: np.asarray(v) for k, v in i.items()}
    blob = np.zeros((C + 1, BLOB), np.float32)
    tables = [f["L0_gnn_W"][0], f["L0_gnn_W"][1], f["L1_gnn_weight"][:C], f["L2_gnn_weight_w"], f["L3_gnn_W"]]
    rest = [f["L0_gnn_mlp_w"][:C], f["L0_gnn_mlp_w"][C:2 * C], f["L1_gnn_weight"][C:], None, None]
    bias = [f["L0_gnn_mlp_b"], None, f["L1_gnn_bias"], f["L2_gnn_bias"], None]
    for l in range(NL):
        blob[:C, l * RC:l * RC + C] = tables[l]
        if rest[l] is not None:
            blob[:C, l * RC + TC:(l + 1) * RC] = rest[l]
        if bias[l] is not None:
            blob[C, l * RC + TC:(l + 1) * RC] = bias[l]
        if l in WT_OF:
            blob[:C, WT + WT_OF[l] * (C + 1):WT + WT_OF[l] * (C + 1) + C] = tables[l].T
    blob[:C, MLP2:MLP2 + C] = f["L0_gnn_mlp_w"][2 * C:]
    for k, a in enumerate((f["L2_gnn_weight_a"], f["L3_gnn_a"])):
        blob[:C, A2 + 2 * k] = a[C:, 0]
        blob[:C, A2 + 2 * k + 1] = a[:C, 0]
    for l in range(2):
        blob[:HID, LT + 2 * l * C:LT + (2 * l + 1) * C] = f["L0_gnn_lin_w"][l, C:].T
        blob[:HID, LT + (2 * l + 1) * C:LT + (2 * l + 2) * C] = f["L0_gnn_lin_w"][l, :C].T
        blob[:HID, AV + l] = f["L0_gnn_attn"][l, :, 0]
        blob[:HID, LB + l * (C + 1) + C] = f["L0_gnn_lin_b"][l]
    return blob


def kernel(x, adj, **weights):
    import concourse.bacc as bacc
    from concourse.bass_utils import run_bass_kernel_spmd

    arrays = {
        "x": np.ascontiguousarray(x),
        "adj": np.ascontiguousarray(adj),
        "weights": packed(weights),
    }
    nc = bacc.Bacc("TRN2", target_bir_lowering=False, num_devices=1)
    args = [nc.dram_tensor(n, a.shape, mybir.dt.from_np(a.dtype), kind="ExternalInput").ap() for n, a in arrays.items()]
    out = nc.dram_tensor("result", (N, C), F32, kind="ExternalOutput").ap()
    build(nc, *args, out)
    return run_bass_kernel_spmd(nc, [arrays], core_ids=[0]).results[0]["result"]
```

```python
from contextlib import ExitStack

import numpy as np

import concourse.bass as bass
from concourse import mybir

F32 = mybir.dt.float32
BF16 = mybir.dt.bfloat16
I32 = mybir.dt.int32
ALU = mybir.AluOpType
ACT = mybir.ActivationFunctionType
AX = mybir.AxisListType.X

P = 128
N = 8192
C = 64
NT = N // P
TC = C + 2
RC = TC + C
UT = 4
NU = NT // UT
NGR = NU
NQ = 4
QC = N // NQ
SLOTS = 16
CH = 5
CAP = CH * P
GW = 1024
GB = N // GW
BIG = 1.0e30
TB = 4
NB = NT // TB
NEG = 9.0e15
EPS = 1e-5
HID = 32
LW = SLOTS + 2
ARENA = 25640
L0_MIX = 0.2

SLOPE = [0.2, 0.2, None, 0.01, 0.2]
NL = len(SLOPE)

MLP2 = NL * RC
WT = MLP2 + C
A2 = WT + 4 * (C + 1)
LT = A2 + 4
AV = LT + 2 * 2 * C
LB = AV + 2
BLOB = LB + 2 * (C + 1)
WT_OF = {0: 0, 1: 1, 3: 2, 4: 3}


class Count:

    def __init__(self, sem):
        self.sem, self.base, self.turn, self.per, self.k = sem, 0, 0, 0, 0

    def loop(self, turn, per):
        self.base, self.turn, self.per, self.k = self.base + self.k, turn, per, 0

    def end(self, turns):
        assert self.k == self.per, (self.k, self.per)
        self.base, self.turn, self.per, self.k = self.base + turns * self.per, 0, 0, 0

    def at(self):
        return self.turn * self.per + (self.base + self.k) if self.per else self.base + self.k


def build(nc, x_in, adj_in, blob_in, out):
    adj_t = adj_in.rearrange("(t p) j -> t p j", p=P)
    with ExitStack() as ctx:
        def sb(name, shape, dt):
            return ctx.enter_context(nc.sbuf_tensor(name, shape, dt))

        def sem(name):
            return ctx.enter_context(nc.semaphore(name))

        x = sb("nodes", [P, NT, C], F32)
        res = sb("res", [P, NT, C], F32)
        hid = sb("hid", [P, NT, C], F32)
        tab = sb("tab", [P, NT, TC], F32)
        own = sb("own", [P, NT], F32)
        w = sb("w", [P, BLOB], F32)
        ident = sb("ident", [P, P], F32)
        ones = sb("ones", [P, P], F32)
        xt = sb("xt", [C + 1, 2, UT * P], F32)
        a2 = sb("a2", [C, 2, 2], F32)
        stat = sb("stat", [P, NT], F32)
        mean = sb("mean", [P, NT], F32)
        adjq = sb("adjq", [P, NQ, QC], I32)
        arena = sb("arena", [P, ARENA], F32)

        class Place:
            at = 0

        def take(n, dt=F32):
            words = n * (2 if dt == BF16 else 4) // 4
            view = arena[:, Place.at:Place.at + words]
            Place.at += words
            assert Place.at <= ARENA, Place.at
            return view if dt == F32 else view.bitcast(dt)

        vb = take(N)
        s = take(2 * N).rearrange("p (a j) -> p a j", a=2)
        pt = take(2 * TB * P).rearrange("p (a j) -> p a j", a=2)
        nmax, rden = take(2), take(2)
        Place.at = 0
        ab = take(2 * N, BF16).rearrange("p (a j) -> p a j", a=2)
        big = arena[:, 0:NT * C].rearrange("p (t c) -> p t c", c=C)
        stage = arena[:, NT * C:NT * C + 2 * UT * C].rearrange("p (b k c) -> p b k c", b=2, c=C)
        keyb = take(GW)
        keys = take(UT * SLOTS).rearrange("p (k s) -> p k s", k=UT)
        ki, gi = take(UT * SLOTS, I32), take(UT * SLOTS, I32)
        bits = take(GB * UT * SLOTS, I32).rearrange("p (b n) -> p b n", b=GB)
        cand = take(UT * GB * SLOTS).rearrange("p (k b s) -> p k b s", k=UT, b=GB)
        dtmp = take(P, BF16)
        valid = take(UT * SLOTS).rearrange("p (k s) -> p k s", k=UT)
        deg4, end4 = take(UT), take(UT)
        lst = take(UT * LW).rearrange("p (k s) -> p k s", k=UT)
        mtmp = take(CAP)
        mf = take(2 * CAP).rearrange("p (a e) -> p a e", a=2)
        oh = take(UT * CH * SLOTS).rearrange("p (e s) -> p e s", s=SLOTS)
        idx1 = take(UT * CH)
        iota = take(CAP)
        gnum = take(GW)
        below = take(P)
        identb = take(P, BF16)
        sid = take(GB * P, BF16).rearrange("p (b c) -> p b c", b=GB)
        posc = take(CH)
        rs = take(NT * NQ).rearrange("p (t r) -> p t r", r=NQ)
        rsum, tot, bad, base_of, endall, deg, dgb = (take(NT) for _ in range(7))
        badn = take(1)
        dg = take(NT)
        vbias = take(NT * SLOTS).rearrange("p (t s) -> p t s", s=SLOTS)
        idx = take(NT * CH, I32)
        rowi, slot = take(NT * CH), take(NT * CH)
        ixs = take(2 * UT * CH, I32).rearrange("p (a e) -> p a e", a=2)
        feat = take(2 * UT * CH * TC).rearrange("p (a e c) -> p a e c", a=2, c=TC)
        st = take(UT * CH * P).rearrange("p (e i) -> p e i", i=P)
        mbt = take(CAP, BF16)
        mb = take(UT * CAP, BF16).rearrange("p (k e) -> p k e", k=UT)
        q = take(UT * CH * SLOTS).rearrange("p (e s) -> p e s", s=SLOTS)
        vs = take(UT * SLOTS).rearrange("p (k s) -> p k s", k=UT)
        vself, vmax, zr, zs, ws = (take(UT) for _ in range(5))
        um = take(2 * UT).rearrange("p (k a) -> p k a", a=2)
        ur = take(2 * UT).rearrange("p (k a) -> p k a", a=2)
        ums = take(6 * UT, BF16).rearrange("p (k s a) -> p k s a", s=3, a=2)
        ue = take(2 * UT * CH).rearrange("p (e a) -> p e a", a=2)
        we = take(UT * CH)
        rd = take(UT)
        part = take(UT * C).rearrange("p (k c) -> p k c", c=C)
        flag = sb("flag", [P, 1], I32)
        ps = ctx.enter_context(nc.psum_tensor("ps", [P, 8, 512], F32))
        sqs = big
        tables = [nc.dram_tensor(f"table{k}", (N, TC), F32, kind="Internal").ap() for k in range(2)]

        x_loaded = sem("x_loaded")
        w_loaded = sem("w_loaded")
        const_made = sem("const_made")
        vec_const = sem("vec_const")
        w_mm = sem("w_mm")
        w_cp = sem("w_cp")
        staged = sem("staged")
        t_turned = sem("t_turned")
        xt_copied = sem("xt_copied")
        proj_done = sem("proj_done")
        proj_used = sem("proj_used")
        nodes_ready = sem("nodes_ready")
        diag_made = sem("diag_made")
        vb_summed = sem("vb_summed")
        vb_ready = sem("vb_ready")
        adj_loaded = [sem(f"adj_loaded{r}") for r in range(NQ)]
        conv_loaded = [sem(f"conv_loaded{r}") for r in range(NQ)]
        sparse_const = sem("sparse_const")
        converted = sem("converted")
        diag_cut = sem("diag_cut")
        folded = sem("folded")
        code_used = sem("code_used")
        keys_ready = sem("keys_ready")
        deg_ready = sem("deg_ready")
        waited_vec = sem("waited_vec")
        waited_pool = sem("waited_pool")
        base_mm = sem("base_mm")
        mf_ready = sem("mf_ready")
        list_mm = sem("list_mm")
        lists_ready = sem("lists_ready")
        bad_ready = sem("bad_ready")
        bad_mm = sem("bad_mm")
        flag_ready = sem("flag_ready")
        build_step = sem("build_step")
        dense_step = sem("dense_step")
        sparse_step = sem("sparse_step")
        table_stored = sem("table_stored")
        idx_staged = sem("idx_staged")
        gathered = [sem("gathered0"), sem("gathered1")]
        st_ready = sem("st_ready")
        mb_ready = sem("mb_ready")
        q_ready = sem("q_ready")
        vp_mm = sem("vp_mm")
        um_ready = sem("um_ready")
        um_mm = sem("um_mm")
        self_in = sem("self_in")
        self_exp = sem("self_exp")
        edge_in = sem("edge_in")
        edge_exp = sem("edge_exp")
        fs_ready = sem("fs_ready")
        sum_mm = sem("sum_mm")
        sum_used = sem("sum_used")
        adj_used = sem("adj_used")
        z_ready = sem("z_ready")
        max_ready = sem("max_ready")
        p_ready = sem("p_ready")
        m_ready = sem("m_ready")
        p_turned = sem("p_turned")
        pt_copied = sem("pt_copied")
        pt_used = sem("pt_used")
        agg_used = sem("agg_used")
        vec_step = sem("vec_step")
        elu_in = sem("elu_in")
        elu_exp = sem("elu_exp")
        var_ready = sem("var_ready")
        std_ready = sem("std_ready")
        out_stored = sem("out_stored")
        block = ctx.enter_context(nc.Block())

        GATS = [l for l in range(NL) if SLOPE[l] is not None]
        STAGES = [0, 1, None, 2, 3, 4]

        def gats_before(l):
            return sum(k < l for k in GATS)

        def stages_before(l):
            return STAGES.index(l)

        @block.sync
        def _(sp):
            sp.dma_start(x[:, :, :], x_in.rearrange("(t p) c -> p t c", p=P)).then_inc(x_loaded, 16)
            sp.dma_start(w[0:C + 1, :], blob_in).then_inc(w_loaded, 16)

            def build_load(t, first):
                for r in range(NQ):
                    if not first:
                        sp.wait_ge(converted, t * NQ + (r + 1 - NQ))
                    sp.dma_start(adjq[:, r, :], adj_t[bass.ds(t, 1), :, r * QC:(r + 1) * QC].rearrange(
                        "a p j -> p (a j)")).then_inc(conv_loaded[r], 16)
            build_load(0, True)
            with sp.Fori(1, NT) as t:
                build_load(t, False)

            sp.wait_ge(flag_ready, 1)
            dense = sp.value_load(flag[0:1, 0:1])
            with sp.If(dense):
                for l in range(NL):
                    def load(t, first):
                        for h in range(NQ):
                            if not first:
                                sp.wait_ge(adj_used, t * NQ + (l * NT * NQ + h + 1 - NQ))
                            sp.dma_start(adjq[:, h, :], adj_t[bass.ds(t, 1), :, h * QC:(h + 1) * QC].rearrange(
                                "a p j -> p (a j)")).then_inc(adj_loaded[h], 16)
                    load(0, l == 0)
                    with sp.Fori(1, NT) as t:
                        load(t, False)
            sp.wait_ge(nodes_ready, NL + 1)
            sp.dma_start(out.rearrange("(t p) c -> p t c", p=P), x[:, :, :]).then_inc(out_stored, 16)
            sp.wait_ge(out_stored, 16)

        @block.gpsimd
        def _(pool):
            pool.memset(ident[:, :], 0.0).then_inc(const_made, 1)
            pool.memset(ones[:, :], 1.0).then_inc(const_made, 1)
            pool.memset(tab[:, :, C + 1:C + 2], 1.0).then_inc(const_made, 1)
            pool.wait_ge(const_made, 3)
            pool.memset(xt[C:C + 1, :, :], 1.0).then_inc(const_made, 1)
            pool.wait_ge(const_made, 4)
            pool.affine_select(out=ident[:, :], in_=ident[:, :], compare_op=ALU.not_equal, fill=1.0,
                               base=0, pattern=[[-1, P]], channel_multiplier=1).then_inc(const_made, 1)
            pool.iota(iota, [[1, CAP]], base=0, channel_multiplier=0,
                      allow_small_or_imprecise_dtypes=True).then_inc(sparse_const, 1)
            pool.iota(gnum, [[1 << GB, GW]], base=0, channel_multiplier=0,
                      allow_small_or_imprecise_dtypes=True).then_inc(sparse_const, 1)
            pool.iota(posc, [[P, CH]], base=0, channel_multiplier=1,
                      allow_small_or_imprecise_dtypes=True).then_inc(sparse_const, 1)
            pool.iota(lst[:, :, SLOTS + 1], [[0, UT]], base=1, channel_multiplier=1,
                      allow_small_or_imprecise_dtypes=True).then_inc(sparse_const, 1)
            pool.memset(identb, 0.0).then_inc(sparse_const, 1)
            pool.memset(sid, 0.0).then_inc(sparse_const, 1)
            pool.memset(below, 1.0).then_inc(sparse_const, 1)
            pool.wait_ge(sparse_const, 7)
            pool.affine_select(out=identb, in_=identb, compare_op=ALU.not_equal, fill=1.0,
                               base=0, pattern=[[-1, P]], channel_multiplier=1).then_inc(sparse_const, 1)
            for b in range(GB):
                pool.affine_select(out=sid[:, b, :], in_=sid[:, b, :], compare_op=ALU.not_equal, fill=float(1 << b),
                                   base=0, pattern=[[-1, P]], channel_multiplier=1).then_inc(sparse_const, 1)
            pool.affine_select(out=below, in_=below, compare_op=ALU.is_gt, fill=0.0,
                               base=0, pattern=[[1, P]], channel_multiplier=-1).then_inc(sparse_const, 1)
            pool.wait_ge(flag_ready, 1)
            dense = pool.value_load(flag[0:1, 0:1])
            for l in range(NL):
                with pool.If(dense):
                    pool.nop()
                with pool.Else():
                    pool.wait_ge(table_stored, 16 * (l + 1))
                    pool.wait_ge(lists_ready, NGR)

                    def gather(g, i, b, first):
                        if not first:
                            pool.wait_ge(gathered[b], i * (16 * UT * CH) + l * (NGR // 2) * 16 * UT * CH)
                            pool.wait_ge(sum_mm, g + (l * NGR - 1))
                        pool.tensor_copy(ixs[:, b, :], idx[:, bass.ds(g * UT * CH, UT * CH)]).then_inc(idx_staged, 1)
                        pool.wait_ge(idx_staged, g + (l * NGR + 1))
                        pool.sem_inc(waited_pool, 1)
                        for e in range(UT * CH):
                            pool.indirect_dma_start(feat[:, b, e, :], None, tables[l % 2],
                                                    bass.IndirectOffsetOnAxis(ap=ixs[:, b, e:e + 1], axis=0)).then_inc(gathered[b], 16)
                    gather(0, 0, 0, l == 0)
                    gather(1, 0, 1, l == 0)
                    with pool.Fori(1, NGR // 2) as i:
                        for b in range(2):
                            gather(2 * i + b, i, b, False)

        @block.tensor
        def _(pe):
            pe.wait_ge(w_loaded, 16)
            pe.wait_ge(const_made, 5)
            for l in range(2):
                for k in range(2):
                    mm = pe.matmul(ps[0:C, 0, 2 * l + k:2 * l + k + 1], w[0:HID, LT + (2 * l + k) * C:LT + (2 * l + k + 1) * C],
                                   w[0:HID, AV + l:AV + l + 1], start=True, stop=True)
            mm.then_inc(w_mm, 1)
            pe.wait_ge(w_cp, 1)
            for l in GATS:
                o = ps[0:C + 1, 1 + WT_OF[l], 0:2]
                rhs = a2[:, l, :] if l < 2 else w[0:C, A2 + 2 * (l - 3):A2 + 2 * (l - 2)]
                lhs = w[0:C, WT + WT_OF[l] * (C + 1):WT + (WT_OF[l] + 1) * (C + 1)]
                mm = pe.matmul(o, lhs, rhs, start=True, stop=(l >= 2))
                if l < 2:
                    mm = pe.matmul(ps[0:C + 1, 1 + WT_OF[l], 1:2], w[0:HID, LB + l * (C + 1):LB + (l + 1) * (C + 1)],
                                   w[0:HID, AV + l:AV + l + 1], start=False, stop=True)
            mm.then_inc(w_mm, 1)
            pe.wait_ge(x_loaded, 16)
            pe.wait_ge(w_cp, 2)

            def turn(base, q, b, first):
                if not first:
                    pe.wait_ge(xt_copied, q + (base - 1))
                pe.wait_ge(staged, q + (base + 1))
                for k in range(UT):
                    mm = pe.matmul(ps[0:C, b, k * P:(k + 1) * P], stage[:, b, k, :], ident[:, :], start=True, stop=True)
                mm.then_inc(t_turned, 1)

            def product(n, base, q, b, first):
                pe.wait_ge(xt_copied, q + (base + 1))
                if not first:
                    pe.wait_ge(proj_used, q + base)
                l = STAGES[n]
                for k in range(UT):
                    o = ps[:, 2 + k // 2, :]
                    lhs = xt[:, b, k * P:(k + 1) * P]
                    if l is None:
                        mm = pe.matmul(o[:, (k % 2) * RC:(k % 2) * RC + C], lhs, w[0:C + 1, MLP2:MLP2 + C],
                                       start=True, stop=True)
                    else:
                        mm = pe.matmul(o[:, (k % 2) * RC:(k % 2 + 1) * RC], lhs, w[0:C + 1, l * RC:(l + 1) * RC],
                                       start=True, stop=True)
                mm.then_inc(proj_done, 1)

            def project(n):
                base = n * NU
                turn(base, 0, 0, n == 0)
                turn(base, 1, 1, n == 0)
                product(n, base, 0, 0, n == 0)
                product(n, base, 1, 1, False)
                with pe.Fori(1, NU // 2) as i:
                    for b in range(2):
                        turn(base, 2 * i + b, b, False)
                    for b in range(2):
                        product(n, base, 2 * i + b, b, False)

            def spread(l):
                base = gats_before(l) * NU
                pe.wait_ge(proj_used, (stages_before(l) + 1) * NU)

                def unit(q, b, first):
                    pe.wait_ge(diag_made, q + (base + 1))
                    if not first:
                        pe.wait_ge(vb_ready, q + (base - 1))
                    pe.matmul(ps[:, b, :], ones[:, :], pt[:, b, :], start=True, stop=True).then_inc(vb_summed, 1)
                unit(0, 0, l == 0)
                unit(1, 1, l == 0)
                with pe.Fori(1, NU // 2) as i:
                    for b in range(2):
                        unit(2 * i + b, b, False)
                pe.wait_ge(vb_ready, base + NU)

            def aggregate(l):
                if SLOPE[l] is not None:
                    spread(l)
                else:
                    pe.wait_ge(proj_used, (stages_before(l) + 1) * NU)

                def tile(t, b, first):
                    if SLOPE[l] is None:
                        pe.wait_ge(m_ready, t + 1)
                    else:
                        pe.wait_ge(p_ready, t + (gats_before(l) * NT + 1))
                    tb = t * NB + l * NT * NB

                    def turned(g):
                        if not (first and g < 2):
                            pe.wait_ge(pt_copied, tb + (g - 1))
                        for k in range(TB):
                            j = g * TB + k
                            mm = pe.transpose(ps[:, g % 2, k * P:(k + 1) * P], s[:, b, j * P:(j + 1) * P], ident[:, :])
                        mm.then_inc(p_turned, 1)

                    def summed(g):
                        pe.wait_ge(pt_copied, tb + (g + 1))
                        for k in range(TB):
                            j = g * TB + k
                            mm = pe.matmul(ps[:, 2 + b, 0:TC], pt[:, g % 2, k * P:(k + 1) * P], tab[:, j, :],
                                           start=(j == 0), stop=(j == NT - 1))
                        mm.then_inc(pt_used, 1)

                    turned(0)
                    if not (l == 0 and isinstance(t, int) and t < 2):
                        pe.wait_ge(agg_used, t + (l * NT - 1))
                    for g in range(NB):
                        if g + 1 < NB:
                            turned(g + 1)
                        summed(g)

                tile(0, 0, l == 0)
                tile(1, 1, False)
                with pe.Fori(1, NT // 2) as i:
                    for b in range(2):
                        tile(2 * i + b, b, False)

            def fold(t, b, first):
                pe.wait_ge(diag_cut, t + 1)
                if not first:
                    pe.wait_ge(code_used, t)
                for k in range(GB):
                    for h in range(2):
                        mm = pe.matmul(ps[:, h, :], sid[:, k, :], ab[:, b, k * GW + h * 512:k * GW + (h + 1) * 512],
                                       start=(k == 0), stop=(k == GB - 1))
                mm.then_inc(folded, 1)

            def lists(g, first):
                pe.wait_ge(deg_ready, g + 1)
                if not first:
                    pe.wait_ge(lists_ready, g)
                pe.matmul(ps[:, 4, 0:UT], below, deg4, start=True, stop=True).then_inc(base_mm, 1)
                for k in range(UT):
                    pe.wait_ge(mf_ready, g * UT + (k + 1))
                    for c in range(CH):
                        mm = pe.matmul(ps[:, 5, (k * CH + c) * LW:(k * CH + c + 1) * LW],
                                       mf[:, k % 2, c * P:(c + 1) * P], lst[:, k, :], start=True, stop=True)
                    mm.then_inc(list_mm, 1)

            def build_group(g, first, last):
                for k in range(UT):
                    if not (last and k == UT - 1):
                        fold(g * UT + (k + 1), (k + 1) % 2, False)
                lists(g, first)

            def sparse(l):
                gat = SLOPE[l] is not None

                def group(g, i, b):
                    n = g + (l * NGR + 1)
                    pe.wait_ge(st_ready, n)
                    if gat:
                        gn = g + (gats_before(l) * NGR + 1)
                        pe.wait_ge(q_ready, gn)
                        for k in range(UT):
                            for c in range(CH):
                                e = k * CH + c
                                mm = pe.matmul(ps[:, 4, k * SLOTS:(k + 1) * SLOTS], st[:, e, :], q[:, e, :],
                                               start=(c == 0), stop=(c == CH - 1))
                        mm.then_inc(vp_mm, 1)
                        pe.wait_ge(mb_ready, gn)
                        pe.wait_ge(um_ready, gn)
                        for k in range(UT):
                            for c in range(CH):
                                e = k * CH + c
                                mm = pe.matmul(ps[:, 5, e * 6:(e + 1) * 6], mb[:, k, c * P:(c + 1) * P],
                                               ums[:, k, :, :].rearrange("p s a -> p (s a)"), start=True, stop=True)
                        mm.then_inc(um_mm, 1)
                        pe.wait_ge(fs_ready, gn)
                    else:
                        pe.wait_ge(gathered[b], i * (16 * UT * CH) + (l * (NGR // 2) + 1) * 16 * UT * CH)
                    if l > 0 or not (isinstance(g, int) and g == 0):
                        pe.wait_ge(sum_used, g + l * NGR)
                    for k in range(UT):
                        for c in range(CH):
                            e = k * CH + c
                            mm = pe.matmul(ps[:, 6, k * TC:(k + 1) * TC], st[:, e, :], feat[:, b, e, :],
                                           start=(c == 0), stop=(c == CH - 1))
                    mm.then_inc(sum_mm, 1)

                group(0, 0, 0)
                group(1, 0, 1)
                with pe.Fori(1, NGR // 2) as i:
                    for b in range(2):
                        group(2 * i + b, i, b)

            project(0)
            pe.wait_ge(proj_used, NU)
            pe.wait_ge(sparse_const, 16 + 1)
            fold(0, 0, True)
            build_group(0, True, False)
            with pe.Fori(1, NGR - 1) as g:
                build_group(g, False, False)
            build_group(NGR - 1, False, True)
            pe.wait_ge(bad_ready, 1)
            pe.matmul(ps[:, 4, 0:1], ones[:, :], badn, start=True, stop=True).then_inc(bad_mm, 1)
            pe.wait_ge(flag_ready, 1)
            dense = pe.value_load(flag[0:1, 0:1])
            for n, l in enumerate(STAGES):
                if n > 0:
                    project(n)
                if l is not None:
                    pe.wait_ge(proj_used, (n + 1) * NU)
                    with pe.If(dense):
                        aggregate(l)
                    with pe.Else():
                        sparse(l)

        @block.scalar
        def _(act):
            def project(n):
                base = n * NU

                src = hid if n in (1, 2) else x

                def put(q, b, first):
                    if not first:
                        act.wait_ge(t_turned, q + (base - 1))
                    act.activation(stage[:, b, :, :], src[:, bass.ds(q * UT, UT), :], ACT.Copy).then_inc(staged, 1)

                def unit(q, b, first):
                    act.wait_ge(t_turned, q + (base + 1))
                    if not first:
                        act.wait_ge(proj_done, q + (base - 1))
                    act.activation(xt[0:C, b, :], ps[0:C, b, :], ACT.Copy).then_inc(xt_copied, 1)

                if n > 0:
                    act.wait_ge(nodes_ready, n)
                else:
                    act.wait_ge(x_loaded, 16)
                put(0, 0, n == 0)
                put(1, 1, n == 0)
                unit(0, 0, n == 0)
                put(2, 0, False)
                unit(1, 1, n == 0)
                with act.Fori(1, NU // 2 - 1) as i:
                    for b in range(2):
                        put(2 * i + (b + 1), 1 - b, False)
                        unit(2 * i + b, b, False)
                put(NU - 1, 1, False)
                unit(NU - 2, 0, False)
                unit(NU - 1, 1, False)

            def aggregate(l):
                gat = SLOPE[l] is not None
                gb = gats_before(l) * NT
                if gat:
                    base = gats_before(l) * NU
                    with act.Fori(0, NU // 2) as i:
                        for b in range(2):
                            act.wait_ge(vb_summed, 2 * i + (base + b + 1))
                            act.activation(vb[:, bass.ds((2 * i + b) * UT * P, UT * P)], ps[:, b, :], ACT.Copy).then_inc(vb_ready, 1)
                    act.wait_ge(vb_ready, base + NU)

                def scores(t, b, first):
                    if not first:
                        act.wait_ge(pt_used, (t + (l * NT - 1)) * NB)
                    act.activation(s[:, b, :], vb[:, :], ACT.Identity, bias=own[:, bass.ds(t, 1)]).then_inc(z_ready, 1)

                def tile(t, b, first):
                    if gat:
                        act.wait_ge(max_ready, t + (gb + 1))
                        act.activation(s[:, b, :], s[:, b, :], ACT.Exp, bias=nmax[:, b:b + 1]).then_inc(p_ready, 1)
                    tb = t * NB + l * NT * NB
                    for g in range(NB):
                        act.wait_ge(p_turned, tb + (g + 1))
                        if not (first and g < 2):
                            act.wait_ge(pt_used, tb + (g - 1))
                        act.activation(pt[:, g % 2, :], ps[:, g % 2, :], ACT.Copy).then_inc(pt_copied, 1)

                if gat:
                    scores(0, 0, True)
                    scores(1, 1, True)
                tile(0, 0, l == 0)
                if gat:
                    scores(2, 0, False)
                tile(1, 1, False)
                with act.Fori(1, NT // 2 - 1) as i:
                    for b in range(2):
                        if gat:
                            scores(2 * i + (b + 1), 1 - b, False)
                        tile(2 * i + b, b, False)
                if gat:
                    scores(NT - 1, 1, False)
                tile(NT - 2, 0, False)
                tile(NT - 1, 1, False)

            def convert(t, b, first):
                for r in range(NQ):
                    act.wait_ge(conv_loaded[r], t * 16 + 16)
                    if r == 0 and not first:
                        act.wait_ge(folded, t - 1)
                    act.activation(ab[:, b, r * QC:(r + 1) * QC], adjq[:, r, :], ACT.Copy,
                                   accum_out=rs[:, bass.ds(t, 1), r]).then_inc(converted, 1)

            def sparse(l):
                gb = gats_before(l) * NGR
                with act.Fori(0, NGR) as g:
                    act.wait_ge(self_in, g + (gb + 1))
                    act.activation(ws, ws, ACT.Exp).then_inc(self_exp, 1)
                    act.wait_ge(edge_in, g + (gb + 1))
                    act.activation(we, we, ACT.Exp).then_inc(edge_exp, 1)

            def store_table(n, l):
                act.wait_ge(proj_used, (n + 1) * NU)
                act.dma_start(tables[l % 2].rearrange("(t p) c -> p t c", p=P), tab[:, :, :]).then_inc(table_stored, 16)

            project(0)
            store_table(0, 0)
            act.wait_ge(table_stored, 16)
            convert(0, 0, True)
            convert(1, 1, True)
            with act.Fori(1, NT // 2) as i:
                for b in range(2):
                    convert(2 * i + b, b, False)
            act.wait_ge(flag_ready, 1)
            dense = act.value_load(flag[0:1, 0:1])
            elus = 0
            lns = 0
            for n, l in enumerate(STAGES):
                if n > 0:
                    project(n)
                    if l is not None:
                        store_table(n, l)
                if l is not None:
                    with act.If(dense):
                        aggregate(l)
                    with act.Else():
                        if SLOPE[l] is not None:
                            sparse(l)
                        else:
                            act.nop()
                if l in (0, 1, 4):
                    elus += 1
                    act.wait_ge(elu_in, elus)
                    act.activation(big, big, ACT.Exp).then_inc(elu_exp, 1)
                if l not in (0, 1):
                    lns += 1
                    act.wait_ge(var_ready, lns)
                    act.activation(stat[:, :], stat[:, :], ACT.Sqrt).then_inc(std_ready, 1)
            act.wait_ge(table_stored, 16 * NL)

        @block.vector
        def _(dve):
            step = Count(vec_step)

            dense_count = Count(dense_step)
            build_count = Count(build_step)
            sparse_count = Count(sparse_step)

            def link(ins, count=step):
                ins.then_inc(count.sem, 1)
                count.k += 1
                dve.wait_ge(count.sem, count.at())

            def dlink(ins):
                link(ins, dense_count)

            def blink(ins):
                link(ins, build_count)

            def slink(ins):
                link(ins, sparse_count)

            dve.wait_ge(w_loaded, 16)
            dve.wait_ge(w_mm, 1)
            dve.tensor_copy(a2[:, :, :], ps[0:C, 0, 0:4].rearrange("p (l k) -> p l k", l=2)).then_inc(w_cp, 1)
            dve.wait_ge(w_mm, 2)
            for l in GATS:
                cp = dve.tensor_copy(w[0:C + 1, l * RC + C:l * RC + TC], ps[0:C + 1, 1 + WT_OF[l], 0:2])
            cp.then_inc(w_cp, 1)
            dve.wait_ge(x_loaded, 16)
            dve.wait_ge(const_made, 5)

            def project(n):
                l = STAGES[n]
                base = n * NU
                if l is not None and l > 0:
                    dve.wait_ge(table_stored, 16 * l)
                with dve.Fori(0, NU // 2) as i:
                    for b in range(2):
                        q = 2 * i + b
                        dve.wait_ge(proj_done, q + (base + 1))
                        r = res[:, bass.ds(q * UT, UT), :].rearrange("p (a k) c -> p a k c", k=2)
                        xs = x[:, bass.ds(q * UT, UT), :].rearrange("p (a k) c -> p a k c", k=2)
                        both = ps[:, 2:4, 0:2 * RC].rearrange("p a (k c) -> p a k c", k=2)
                        if l is None:
                            dve.tensor_tensor(r, both[:, :, :, 0:C], r, ALU.add).then_inc(proj_used, 1)
                            continue
                        dve.tensor_copy(tab[:, bass.ds(q * UT, UT), 0:C + 1].rearrange("p (a k) c -> p a k c", k=2),
                                        both[:, :, :, 0:C + 1])
                        dve.tensor_copy(own[:, bass.ds(q * UT, UT)].rearrange("p (a k) -> p a k", k=2),
                                        both[:, :, :, C + 1])
                        dve.tensor_tensor(r, both[:, :, :, TC:RC], r if n == 1 else xs, ALU.add).then_inc(proj_used, 1)
                dve.wait_ge(proj_used, base + NU)

            def aggregate(l):
                gat = SLOPE[l] is not None
                if gat:
                    base = gats_before(l) * NU

                    def diagonals(q, b, first):
                        if not first:
                            dve.wait_ge(vb_summed, q + (base - 1))
                        for k in range(UT):
                            d = dve.tensor_scalar(pt[:, b, k * P:(k + 1) * P], ident[:, :],
                                                  tab[:, bass.ds(q * UT + k, 1), C:C + 1].rearrange(
                                                      "p a c -> p (a c)"), None, ALU.mult)
                        d.then_inc(diag_made, 1)
                    diagonals(0, 0, l == 0)
                    diagonals(1, 1, l == 0)
                    with dve.Fori(1, NU // 2) as i:
                        for b in range(2):
                            diagonals(2 * i + b, b, False)

                def edges(t, b):
                    if gat:
                        dve.wait_ge(z_ready, t + (gats_before(l) * NT + 1))
                        dlink(dve.scalar_tensor_tensor(out=s[:, b, :], in0=s[:, b, :], scalar=SLOPE[l], in1=s[:, b, :],
                                                      op0=ALU.mult, op1=ALU.max))
                    elif not (isinstance(t, int) and t < 2):
                        dve.wait_ge(pt_used, (t + (l * NT - 1)) * NB)
                    for h in range(NQ):
                        dve.wait_ge(adj_loaded[h], t * 16 + (l * NT + 1) * 16)
                        sh = s[:, b, h * QC:(h + 1) * QC]
                        if gat:
                            m = adjq[:, h, :].bitcast(F32)
                            dlink(dve.tensor_scalar(m, adjq[:, h, :], 0, NEG, ALU.is_gt, ALU.mult))
                            dve.scalar_tensor_tensor(out=sh, in0=m, scalar=-NEG, in1=sh,
                                                     op0=ALU.add, op1=ALU.add).then_inc(adj_used, 1)
                        else:
                            dve.tensor_scalar(sh, adjq[:, h, :], 1, None, ALU.is_equal).then_inc(adj_used, 1)
                    dve.wait_ge(adj_used, t * NQ + (l * NT * NQ + NQ))
                    if gat:
                        dve.tensor_reduce(nmax[:, b:b + 1], s[:, b, :], AX, ALU.max, negate=True).then_inc(max_ready, 1)
                    else:
                        dve.tensor_copy(nmax[:, b:b + 1], ones[:, 0:1]).then_inc(m_ready, 1)

                def divided(t, b):
                    dve.wait_ge(pt_used, (t + (l * NT + 1)) * NB)
                    dlink(dve.reciprocal(rden[:, b:b + 1], ps[:, 2 + b, C + 1:TC]))
                    dve.tensor_scalar(hid[:, bass.ds(t, 1), :].rearrange("p a c -> p (a c)"), ps[:, 2 + b, 0:C],
                                      rden[:, b:b + 1], None, ALU.mult).then_inc(agg_used, 1)

                edges(0, 0)
                edges(1, 1)
                divided(0, 0)
                with dve.Fori(1, NT // 2) as i:
                    dense_count.loop(i - 1, 2 * (2 + NQ if gat else 1))
                    for b in range(2):
                        edges(2 * i + b, b)
                        divided(2 * i + (b - 1), 1 - b)
                    dense_count.end(NT // 2 - 1)
                divided(NT - 1, 1)
                dve.wait_ge(agg_used, (l + 1) * NT)

            def cut_diagonal(t, b):
                dve.wait_ge(converted, t * NQ + NQ)
                if not (isinstance(t, int) and t == 0):
                    dve.wait_ge(diag_cut, t)
                blk = ab[:, b, bass.ds(t * P, P)]
                blink(dve.scalar_tensor_tensor(out=dtmp, in0=blk, scalar=1.0, in1=identb, op0=ALU.mult, op1=ALU.mult,
                                               accum_out=dg[:, bass.ds(t, 1)]))
                dve.tensor_tensor(blk, blk, dtmp, ALU.subtract).then_inc(diag_cut, 1)

            def settled():
                dve.sem_inc(waited_vec, 1)

            def code_keys(t, k):
                dve.wait_ge(folded, t + 1)
                if not (isinstance(t, int) and t == 0):
                    dve.wait_ge(keys_ready, t)
                code = ps[:, 0:2, :].rearrange("p h g -> p (h g)")
                blink(dve.scalar_tensor_tensor(out=keyb, in0=code, scalar=0.0, in1=gnum, op0=ALU.is_gt, op1=ALU.mult))
                dve.tensor_tensor(keyb, keyb, code, ALU.add).then_inc(code_used, 1)
                dve.wait_ge(code_used, t + 1)
                settled()
                blink(dve.max(keys[:, k, 0:8], keyb))
                settled()
                blink(dve.match_replace(keyb, keys[:, k, 0:8], keyb, 0.0))
                settled()
                dve.max(keys[:, k, 8:16], keyb).then_inc(keys_ready, 1)

            def build_lists(g):
                n = bass.ds(g * UT, UT)
                ne = bass.ds(g * UT * CH, UT * CH)
                dve.wait_ge(keys_ready, g * UT + UT)
                blink(dve.tensor_copy(ki, keys.rearrange("p k s -> p (k s)")))
                dve.tensor_scalar(gi, ki, GB, GW - 1, ALU.logical_shift_right, ALU.bitwise_and)
                for b in range(GB):
                    bit = dve.tensor_scalar(bits[:, b, :], ki, b, 1, ALU.logical_shift_right, ALU.bitwise_and)
                blink(bit)
                for b in range(GB):
                    c = dve.scalar_tensor_tensor(out=cand[:, :, b, :], in0=gi.rearrange("p (k s) -> p k s", k=UT),
                                                 scalar=float(GW * b + 1), in1=bits[:, b, :].rearrange("p (k s) -> p k s", k=UT),
                                                 op0=ALU.add, op1=ALU.mult)
                blink(c)
                settled()
                flat = [cand[:, k, :, :].rearrange("p b s -> p (b s)") for k in range(UT)]
                for k in range(UT):
                    m = dve.max(lst[:, k, 0:8], flat[k])
                blink(m)
                settled()
                for k in range(UT):
                    m = dve.match_replace(flat[k], lst[:, k, 0:8], flat[k], 0.0)
                blink(m)
                settled()
                for k in range(UT):
                    m = dve.max(lst[:, k, 8:16], flat[k])
                blink(m)
                blink(dve.tensor_scalar(valid, lst[:, :, 0:SLOTS], 0.0, None, ALU.is_gt))
                dve.tensor_scalar(vbias[:, n, :], valid, -1.0, BIG, ALU.add, ALU.mult)
                dve.tensor_reduce(deg4, valid, AX, ALU.add).then_inc(deg_ready, 1)
                dve.wait_ge(base_mm, g + 1)
                base = ps[:, 4, 0:UT]
                dve.tensor_copy(lst[:, :, SLOTS], base)
                dve.tensor_copy(deg[:, n], deg4)
                dve.tensor_copy(base_of[:, n], base)
                dve.tensor_tensor(endall[:, n], base, deg4, ALU.add)
                blink(dve.tensor_tensor(end4, base, deg4, ALU.add))
                for k in range(UT):
                    if k > 0:
                        dve.wait_ge(mf_ready, g * UT + k)
                    blink(dve.tensor_scalar(mtmp, iota, lst[:, k, SLOTS:SLOTS + 1], None, ALU.is_ge))
                    if k >= 2:
                        dve.wait_ge(list_mm, g * UT + (k - 1))
                    dve.scalar_tensor_tensor(out=mf[:, k % 2, :], in0=iota, scalar=end4[:, k:k + 1], in1=mtmp,
                                             op0=ALU.is_lt, op1=ALU.mult).then_inc(mf_ready, 1)
                dve.wait_ge(list_mm, g * UT + UT)
                rows = ps[:, 5, 0:UT * CH * LW].rearrange("p (e s) -> p e s", s=LW)
                dve.tensor_scalar(rowi[:, ne], rows[:, :, SLOTS + 1], -1.0, None, ALU.add)
                blink(dve.tensor_tensor(slot[:, ne].rearrange("p (k c) -> p k c", k=UT),
                                        posc.unsqueeze(1).to_broadcast([P, UT, CH]),
                                        rows[:, :, SLOTS].rearrange("p (k c) -> p k c", k=UT), ALU.subtract))
                all3 = [P, UT * CH, SLOTS]
                blink(dve.tensor_tensor(oh, iota[:, 0:SLOTS].unsqueeze(1).to_broadcast(all3),
                                        slot[:, ne].unsqueeze(2).to_broadcast(all3), ALU.is_equal))
                blink(dve.tensor_tensor(oh, oh, rows[:, :, 0:SLOTS], ALU.mult))
                blink(dve.tensor_reduce(idx1, oh, AX, ALU.add))
                blink(dve.tensor_scalar(idx1, idx1, 1.0, float(N), ALU.max, ALU.min))
                dve.tensor_scalar(idx[:, ne], idx1, -1.0, None, ALU.add).then_inc(lists_ready, 1)

            def judged():
                dve.wait_ge(lists_ready, NGR)
                dve.tensor_reduce(rsum, rs, AX, ALU.add)
                blink(dve.tensor_tensor(tot, deg, dg, ALU.add))
                blink(dve.tensor_tensor(bad, tot, rsum, ALU.not_equal))
                blink(dve.scalar_tensor_tensor(out=bad, in0=tot, scalar=1.0, in1=bad, op0=ALU.is_lt, op1=ALU.add))
                blink(dve.scalar_tensor_tensor(out=bad, in0=endall, scalar=float(CAP), in1=bad, op0=ALU.is_gt, op1=ALU.add))
                dve.tensor_scalar(dgb, dg, -1.0, BIG, ALU.add, ALU.mult)
                dve.tensor_reduce(badn, bad, AX, ALU.add).then_inc(bad_ready, 1)
                dve.wait_ge(bad_mm, 1)
                dve.tensor_copy(flag[:, :], ps[:, 4, 0:1]).then_inc(flag_ready, 1)

            def build_group(g, last):
                for k in range(UT):
                    if not (last and k == UT - 1):
                        cut_diagonal(g * UT + (k + 1), (k + 1) % 2)
                    code_keys(g * UT + k, k)
                build_lists(g)

            def sparse(l):
                gat = SLOPE[l] is not None
                gb = gats_before(l) * NGR

                def group(g, i, b, first):
                    n = bass.ds(g * UT, UT)
                    all_c = [P, UT, C]
                    if not first:
                        dve.wait_ge(sum_mm, g + l * NGR)
                    for e in range(UT * CH):
                        o = dve.tensor_scalar(st[:, e, :], iota[:, 0:P], rowi[:, bass.ds(g * UT * CH + e, 1)], None,
                                              ALU.is_equal)
                    o.then_inc(st_ready, 1)
                    if gat:
                        gn = g + (gb + 1)
                        for k in range(UT):
                            slink(dve.tensor_scalar(mbt, iota, base_of[:, bass.ds(g * UT + k, 1)], None, ALU.is_ge))
                            m = dve.scalar_tensor_tensor(out=mb[:, k, :], in0=iota, scalar=endall[:, bass.ds(g * UT + k, 1)],
                                                         in1=mbt, op0=ALU.is_lt, op1=ALU.mult)
                            if k < UT - 1:
                                slink(m)
                        m.then_inc(mb_ready, 1)
                        dve.wait_ge(gathered[b], i * (16 * UT * CH) + (l * (NGR // 2) + 1) * 16 * UT * CH)
                        f = feat[:, b, :, :]
                        for e in range(UT * CH):
                            o = dve.tensor_scalar(q[:, e, :], iota[:, 0:SLOTS], slot[:, bass.ds(g * UT * CH + e, 1)],
                                                  f[:, e, C:C + 1], ALU.is_equal, ALU.mult)
                        o.then_inc(q_ready, 1)
                        vown, u = tab[:, n, C], own[:, n]
                        dve.tensor_tensor(vself, vown, dgb[:, n], ALU.add)
                        dve.wait_ge(vp_mm, gn)
                        slink(dve.tensor_tensor(vs, ps[:, 4, 0:UT * SLOTS].rearrange("p (k s) -> p k s", k=UT),
                                                vbias[:, n, :], ALU.add))
                        slink(dve.tensor_reduce(vmax, vs, AX, ALU.max))
                        slink(dve.tensor_tensor(vmax, vmax, vself, ALU.max))
                        slink(dve.tensor_tensor(zr, u, vmax, ALU.add))
                        dve.scalar_tensor_tensor(out=um[:, :, 1], in0=zr, scalar=SLOPE[l], in1=zr,
                                                 op0=ALU.mult, op1=ALU.max)
                        slink(dve.tensor_copy(um[:, :, 0], u))
                        slink(dve.tensor_copy(ums[:, :, 0, :], um))
                        slink(dve.tensor_tensor(ur, um, ums[:, :, 0, :], ALU.subtract))
                        slink(dve.tensor_copy(ums[:, :, 1, :], ur))
                        slink(dve.tensor_tensor(ur, ur, ums[:, :, 1, :], ALU.subtract))
                        dve.tensor_copy(ums[:, :, 2, :], ur).then_inc(um_ready, 1)
                        slink(dve.tensor_tensor(zs, u, vown, ALU.add))
                        slink(dve.scalar_tensor_tensor(out=zs, in0=zs, scalar=SLOPE[l], in1=zs, op0=ALU.mult, op1=ALU.max))
                        slink(dve.tensor_tensor(zs, zs, um[:, :, 1], ALU.subtract))
                        dve.tensor_scalar(ws, zs, 0.0, None, ALU.min).then_inc(self_in, 1)
                        dve.wait_ge(um_mm, gn)
                        slink(dve.tensor_reduce(ue, ps[:, 5, 0:UT * CH * 6].rearrange("p (e s a) -> p e a s", s=3, a=2),
                                                AX, ALU.add))
                        slink(dve.tensor_tensor(we, ue[:, :, 0], f[:, :, C], ALU.add))
                        slink(dve.scalar_tensor_tensor(out=we, in0=we, scalar=SLOPE[l], in1=we, op0=ALU.mult, op1=ALU.max))
                        slink(dve.tensor_tensor(we, we, ue[:, :, 1], ALU.subtract))
                        dve.tensor_scalar(we, we, 0.0, None, ALU.min).then_inc(edge_in, 1)
                        dve.wait_ge(edge_exp, gn)
                        dve.tensor_tensor(f, f, we.unsqueeze(2).to_broadcast([P, UT * CH, TC]), ALU.mult).then_inc(fs_ready, 1)
                        slink(dve.tensor_tensor(ws, ws, dg[:, n], ALU.mult))
                        wself = ws
                    else:
                        wself = dg[:, n]
                    if not first:
                        dve.wait_ge(sum_used, g + l * NGR)
                    dve.tensor_tensor(part, tab[:, n, 0:C], wself.unsqueeze(2).to_broadcast(all_c), ALU.mult)
                    dve.wait_ge(sum_mm, g + (l * NGR + 1))
                    sums = ps[:, 6, 0:UT * TC].rearrange("p (k c) -> p k c", k=UT)
                    slink(dve.tensor_tensor(rd, sums[:, :, C + 1], wself, ALU.add))
                    slink(dve.reciprocal(rd, rd))
                    slink(dve.tensor_tensor(part, part, sums[:, :, 0:C], ALU.add))
                    dve.tensor_tensor(hid[:, n, :], part, rd.unsqueeze(2).to_broadcast(all_c), ALU.mult).then_inc(sum_used, 1)

                per = 3 + (2 * UT + 16 if gat else 0)
                group(0, 0, 0, l == 0)
                group(1, 0, 1, False)
                with dve.Fori(1, NGR // 2) as i:
                    sparse_count.loop(i - 1, 2 * per)
                    for b in range(2):
                        group(2 * i + b, i, b, False)
                    sparse_count.end(NGR // 2 - 1)
                dve.wait_ge(sum_used, (l + 1) * NGR)

            def elu(k):
                e = big
                dve.tensor_scalar(e, hid[:, :, :], 0.0, None, ALU.min).then_inc(elu_in, 1)
                dve.wait_ge(elu_exp, k)
                link(dve.scalar_tensor_tensor(out=hid[:, :, :], in0=hid[:, :, :], scalar=0.0, in1=e,
                                              op0=ALU.max, op1=ALU.add))

            def mixed():
                link(dve.tensor_scalar(big, x[:, :, :], L0_MIX, L0_MIX - 1.0, ALU.mult, ALU.add))
                dve.scalar_tensor_tensor(out=hid[:, :, :], in0=hid[:, :, :], scalar=1.0 - L0_MIX, in1=big,
                                         op0=ALU.mult, op1=ALU.add).then_inc(nodes_ready, 1)

            def normed(k):
                bc = [P, NT, C]
                link(dve.tensor_reduce(mean[:, :], res[:, :, :], AX, ALU.add))
                link(dve.tensor_scalar(mean[:, :], mean[:, :], -1.0 / C, None, ALU.mult))
                link(dve.tensor_tensor(res[:, :, :], res[:, :, :], mean[:, :].unsqueeze(2).to_broadcast(bc), ALU.add))
                link(dve.tensor_tensor(sqs, res[:, :, :], res[:, :, :], ALU.mult))
                link(dve.tensor_reduce(stat[:, :], sqs, AX, ALU.add))
                dve.tensor_scalar(stat[:, :], stat[:, :], 1.0 / C, EPS, ALU.mult, ALU.add).then_inc(var_ready, 1)
                dve.wait_ge(std_ready, k)
                link(dve.reciprocal(mean[:, :], stat[:, :]))
                dve.tensor_tensor(x[:, :, :], res[:, :, :], mean[:, :].unsqueeze(2).to_broadcast(bc),
                                  ALU.mult).then_inc(nodes_ready, 1)

            def aggregated(l):
                with dve.If(dense):
                    aggregate(l)
                with dve.Else():
                    sparse(l)

            project(0)
            dve.wait_ge(sparse_const, 17)
            cut_diagonal(0, 0)
            build_group(0, False)
            with dve.Fori(1, NGR - 1) as g:
                per = build_count.k - 1
                build_count.loop(g - 1, per)
                build_group(g, False)
                build_count.end(NGR - 2)
            build_group(NGR - 1, True)
            judged()
            dve.wait_ge(flag_ready, 1)
            dense = dve.value_load(flag[0:1, 0:1])
            aggregated(0)
            elu(1)
            mixed()
            project(1)
            aggregated(1)
            elu(2)
            mixed()
            project(2)
            normed(1)
            for l in (2, 3, 4):
                dve.wait_ge(nodes_ready, l + 1)
                project(l + 1)
                aggregated(l)
                if l == 4:
                    elu(3)
                    link(dve.scalar_tensor_tensor(out=res[:, :, :], in0=hid[:, :, :], scalar=-1.0, in1=res[:, :, :],
                                                  op0=ALU.add, op1=ALU.add))
                else:
                    link(dve.tensor_tensor(res[:, :, :], hid[:, :, :], res[:, :, :], ALU.add))
                normed(l)


def packed(i):
    f = {k: np.asarray(v) for k, v in i.items()}
    blob = np.zeros((C + 1, BLOB), np.float32)
    tables = [f["L0_gnn_W"][0], f["L0_gnn_W"][1], f["L1_gnn_weight"][:C], f["L2_gnn_weight_w"], f["L3_gnn_W"]]
    rest = [f["L0_gnn_mlp_w"][:C], f["L0_gnn_mlp_w"][C:2 * C], f["L1_gnn_weight"][C:], None, None]
    bias = [f["L0_gnn_mlp_b"], None, f["L1_gnn_bias"], f["L2_gnn_bias"], None]
    for l in range(NL):
        blob[:C, l * RC:l * RC + C] = tables[l]
        if rest[l] is not None:
            blob[:C, l * RC + TC:(l + 1) * RC] = rest[l]
        if bias[l] is not None:
            blob[C, l * RC + TC:(l + 1) * RC] = bias[l]
        if l in WT_OF:
            blob[:C, WT + WT_OF[l] * (C + 1):WT + WT_OF[l] * (C + 1) + C] = tables[l].T
    blob[:C, MLP2:MLP2 + C] = f["L0_gnn_mlp_w"][2 * C:]
    for k, a in enumerate((f["L2_gnn_weight_a"], f["L3_gnn_a"])):
        blob[:C, A2 + 2 * k] = a[C:, 0]
        blob[:C, A2 + 2 * k + 1] = a[:C, 0]
    for l in range(2):
        blob[:HID, LT + 2 * l * C:LT + (2 * l + 1) * C] = f["L0_gnn_lin_w"][l, C:].T
        blob[:HID, LT + (2 * l + 1) * C:LT + (2 * l + 2) * C] = f["L0_gnn_lin_w"][l, :C].T
        blob[:HID, AV + l] = f["L0_gnn_attn"][l, :, 0]
        blob[:HID, LB + l * (C + 1) + C] = f["L0_gnn_lin_b"][l]
    return blob


def kernel(x, adj, **weights):
    import concourse.bacc as bacc
    from concourse.bass_utils import run_bass_kernel_spmd

    arrays = {
        "x": np.ascontiguousarray(x),
        "adj": np.ascontiguousarray(adj),
        "weights": packed(weights),
    }
    nc = bacc.Bacc("TRN2", target_bir_lowering=False, num_devices=1)
    args = [nc.dram_tensor(n, a.shape, mybir.dt.from_np(a.dtype), kind="ExternalInput").ap() for n, a in arrays.items()]
    out = nc.dram_tensor("result", (N, C), F32, kind="ExternalOutput").ap()
    build(nc, *args, out)
    return run_bass_kernel_spmd(nc, [arrays], core_ids=[0]).results[0]["result"]
```

```python
from contextlib import ExitStack

import numpy as np

import concourse.bass as bass
from concourse import mybir

F32 = mybir.dt.float32
BF16 = mybir.dt.bfloat16
I32 = mybir.dt.int32
ALU = mybir.AluOpType
ACT = mybir.ActivationFunctionType
AX = mybir.AxisListType.X

P = 128
N = 8192
C = 64
NT = N // P
TC = C + 2
TW = TC + 3
RC = TC + C
UT = 4
NU = NT // UT
NGR = NU
NQ = 4
QC = N // NQ
SLOTS = 16
FULL = 4
CAP = FULL * P + P // 2
CH = FULL + 1
NE = UT * FULL + UT // 2
GW = 1024
GB = N // GW
LOG_GW = GW.bit_length() - 1
GLOW = 32
BIG = 1.0e30
TB = 4
NB = NT // TB
NEG = 9.0e15
EPS = 1e-5
HID = 32
LW = SLOTS + 2
ARENA = 25704
L0_MIX = 0.2

SLOPE = [0.2, 0.2, None, 0.01, 0.2]
NL = len(SLOPE)

MLP2 = NL * RC
WT = MLP2 + C
A2 = WT + 4 * (C + 1)
LT = A2 + 4
AV = LT + 2 * 2 * C
LB = AV + 2
BLOB = LB + 2 * (C + 1)
WT_OF = {0: 0, 1: 1, 3: 2, 4: 3}


class Count:

    def __init__(self, sem):
        self.sem, self.base, self.turn, self.per, self.k = sem, 0, 0, 0, 0

    def start(self, base, turn, per):
        assert self.k == self.per, (self.k, self.per)
        self.base, self.turn, self.per, self.k = base, turn, per, 0

    def at(self):
        return self.turn * self.per + (self.base + self.k)


def build(nc, x_in, adj_in, blob_in, out):
    adj_t = adj_in.rearrange("(t p) j -> t p j", p=P)
    with ExitStack() as ctx:
        def sb(name, shape, dt):
            return ctx.enter_context(nc.sbuf_tensor(name, shape, dt))

        def sem(name):
            return ctx.enter_context(nc.semaphore(name))

        x = sb("nodes", [P, NT, C], F32)
        res = sb("res", [P, NT, C], F32)
        hid = sb("hid", [P, NT, C], F32)
        tab = sb("tab", [P, NT, TW], F32)
        own = sb("own", [P, NT], F32)
        w = sb("w", [P, BLOB], F32)
        ident = sb("ident", [P, P], F32)
        xt = sb("xt", [C + 1, 2, UT * P], F32)
        a2 = sb("a2", [C, 2, 2], F32)
        adjq = sb("adjq", [P, NQ, QC], I32)
        arena = sb("arena", [P, ARENA], F32)

        class Place:
            at = 0

        def take(n, dt=F32):
            words = n * (2 if dt == BF16 else 4) // 4
            view = arena[:, Place.at:Place.at + words]
            Place.at += words
            assert Place.at <= ARENA, Place.at
            return view if dt == F32 else view.bitcast(dt)

        vb = take(N)
        s = take(2 * N).rearrange("p (a j) -> p a j", a=2)
        pt = take(2 * TB * P).rearrange("p (a j) -> p a j", a=2)
        nmax, rden = take(2), take(2)
        Place.at = 0
        ab = take(2 * N, BF16).rearrange("p (a j) -> p a j", a=2)
        keyb = take(GW)
        keys = take(UT * SLOTS).rearrange("p (k s) -> p k s", k=UT)
        ki, gi = take(UT * SLOTS, I32), take(UT * SLOTS, I32)
        bits = take(GB * UT * SLOTS, I32).rearrange("p (b n) -> p b n", b=GB)
        cand = take(UT * GB * SLOTS).rearrange("p (k b s) -> p k b s", k=UT, b=GB)
        dtmp = take(P, BF16)
        valid = take(UT * SLOTS).rearrange("p (k s) -> p k s", k=UT)
        deg4, end4 = take(UT), take(UT)
        lst = take(UT * LW).rearrange("p (k s) -> p k s", k=UT)
        lstb = take(2 * UT * LW, BF16).rearrange("p (a k s) -> p a k s", a=2, k=UT)
        mtmp = take(CH * P)
        mf = take(2 * CH * P, BF16).rearrange("p (a e) -> p a e", a=2)
        oh = take(NE * SLOTS).rearrange("p (e s) -> p e s", s=SLOTS)
        idx1 = take(NE)
        number = take(2 * CH * P).rearrange("p (a e) -> p a e", a=2)
        iota = number[:, 0, 0:FULL * P]
        gnum = take(2 * GW, BF16).rearrange("p (a g) -> p a g", a=2)
        oneb = take(P, BF16)
        below = take(P)
        identb = take(P, BF16)
        sid = take(GB * P, BF16).rearrange("p (b c) -> p b c", b=GB)
        posc, whose = take(NE), take(2)
        ones = take(P)
        rs = take(NT * NQ).rearrange("p (t r) -> p t r", r=NQ)
        rsum, tot, bad, endall, deg, dgb = (take(NT) for _ in range(6))
        badn = take(1)
        dg = take(NT)
        vbias = take(NT * SLOTS).rearrange("p (t s) -> p t s", s=SLOTS)
        idx, slot = take(NGR * NE, I32), take(NGR * NE)
        rowi = take(NT * CH).rearrange("p (t c) -> p t c", c=CH)
        ixs = take(2 * NE, I32).rearrange("p (a e) -> p a e", a=2)
        feat = take(2 * NE * TW).rearrange("p (a e c) -> p a e c", a=2, c=TW)
        lists_end, Place.at = Place.at, 0
        mb = take(UT * CH * P, BF16)
        st = take(2 * UT * CH * P, BF16).rearrange("p (a e i) -> p a e i", a=2, i=P)
        stf = take(UT * CH * P).rearrange("p (e i) -> p e i", i=P)
        fs = take(NE * TC).rearrange("p (e c) -> p e c", c=TC)
        assert Place.at <= 2 * N // 2, Place.at
        Place.at = lists_end
        iotab = take(P, BF16)
        q = take(NE * SLOTS, BF16).rearrange("p (e s) -> p e s", s=SLOTS)
        qv = take(NE * SLOTS * 3, BF16).rearrange("p (e s r) -> p e s r", s=SLOTS, r=3)
        vs = take(UT * SLOTS)
        ues = take(NE * 2).rearrange("p (e a) -> p e a", a=2)
        mrow, mtmp3 = take(UT), take(UT)
        vself, vmax, zr, zs, ws = (take(UT) for _ in range(5))
        um = take(2 * UT * 3, BF16).rearrange("p (k a r) -> p k a r", a=2, r=3)
        we = take(NE)
        rd = take(UT)
        part = take(UT * C).rearrange("p (k c) -> p k c", c=C)
        flag = sb("flag", [P, 1], I32)
        stage = take(2 * UT * C).rearrange("p (b k c) -> p b k c", b=2, c=C)
        eb, sq = (take(UT * C).rearrange("p (k c) -> p k c", c=C) for _ in range(2))
        mean, var, yr, yt = (take(UT) for _ in range(4))
        yi = take(UT, I32)
        ps = ctx.enter_context(nc.psum_tensor("ps", [P, 8, 512], F32))
        tables = [nc.dram_tensor(f"table{k}", (N, TW), F32, kind="Internal").ap() for k in range(2)]

        x_loaded = sem("x_loaded")
        w_loaded = sem("w_loaded")
        const_made = sem("const_made")
        w_mm = sem("w_mm")
        w_cp = sem("w_cp")
        staged = sem("staged")
        t_turned = sem("t_turned")
        xt_copied = sem("xt_copied")
        proj_done = sem("proj_done")
        proj_used = sem("proj_used")
        nodes_ready = sem("nodes_ready")
        ones_made = sem("ones_made")
        diag_made = sem("diag_made")
        vb_summed = sem("vb_summed")
        vb_ready = sem("vb_ready")
        adj_loaded = [sem(f"adj_loaded{r}") for r in range(NQ)]
        conv_loaded = [sem(f"conv_loaded{r}") for r in range(NQ)]
        sparse_const = sem("sparse_const")
        whose_made = sem("whose_made")
        converted = sem("converted")
        diag_cut = sem("diag_cut")
        folded = sem("folded")
        code_used = sem("code_used")
        keys_ready = sem("keys_ready")
        deg_ready = sem("deg_ready")
        waited_vec = sem("waited_vec")
        waited_pool = sem("waited_pool")
        base_mm = sem("base_mm")
        mf_ready = sem("mf_ready")
        list_mm = sem("list_mm")
        lists_ready = sem("lists_ready")
        bad_ready = sem("bad_ready")
        bad_mm = sem("bad_mm")
        flag_ready = sem("flag_ready")
        build_step = sem("build_step")
        dense_step = sem("dense_step")
        sparse_step = sem("sparse_step")
        table_stored = sem("table_stored")
        idx_staged = sem("idx_staged")
        gathered = [sem("gathered0"), sem("gathered1")]
        st_ready = sem("st_ready")
        q_made = sem("q_made")
        q_ready = sem("q_ready")
        vp_mm = sem("vp_mm")
        um_ready = sem("um_ready")
        um_mm = sem("um_mm")
        mt_turned = sem("mt_turned")
        mb_copied = sem("mb_copied")
        epi_step = sem("epi_step")
        self_in = sem("self_in")
        self_exp = sem("self_exp")
        edge_in = sem("edge_in")
        edge_exp = sem("edge_exp")
        stf_ready = sem("stf_ready")
        fs_ready = sem("fs_ready")
        score_step = sem("score_step")
        table_ready = sem("table_ready")
        half_sum_mm = sem("half_sum_mm")
        sum_mm = sem("sum_mm")
        sum_used = sem("sum_used")
        adj_used = sem("adj_used")
        z_ready = sem("z_ready")
        max_ready = sem("max_ready")
        p_ready = sem("p_ready")
        m_ready = sem("m_ready")
        p_turned = sem("p_turned")
        pt_copied = sem("pt_copied")
        pt_used = sem("pt_used")
        agg_used = sem("agg_used")
        vec_step = sem("vec_step")
        second_step = sem("second_step")
        elu_in = sem("elu_in")
        elu_exp = sem("elu_exp")
        out_stored = sem("out_stored")
        block = ctx.enter_context(nc.Block())

        GATS = [l for l in range(NL) if SLOPE[l] is not None]
        ELUS = [0, 1, 4]
        LAYER_OF = {0: 0, 1: 1, 2: None, 3: 2, 4: 3, 5: 4}
        AFTER = {0: [1], 1: [2, 3], 2: [4], 3: [5], 4: [6]}

        def gats_before(l):
            return sum(k < l for k in GATS)

        def unit_no(n, g):
            return {0: g, 1: g + NGR, 2: g * 2 + 2 * NGR, 3: g * 2 + (2 * NGR + 1)}[n] if n < 4 else g + n * NGR

        def buffer_of(n, b):
            return n - 2 if n in (2, 3) else b

        def has(g):
            return not isinstance(g, int) or 0 <= g < NGR

        def pipelined(eng, turn_of, lag):
            for g in range(4):
                turn_of(g, g // 2, g % 2)
            with eng.Fori(2, NGR // 2 - 1) as i:
                for b in range(2):
                    turn_of(2 * i + b, i, b)
            for g in range(NGR - 2, NGR + lag):
                turn_of(g, g // 2, g % 2)

        FILLED = 16
        SPARSE_CONSTS = FILLED + 1 + GB + 1

        SECOND = UT * SLOTS * 3

        PE_LAG = [2, 3, 2, 2, 0]
        ACT_LAG = [2, 3, 2, 2, 1]
        VEC_LAG = [2, 3, 2, 2, 1]

        def elu_no(l, g):
            return g + ELUS.index(l) * NGR

        def product_of(n):
            banks, at = (slice(4, 7, 2), 512 - 2 * RC) if n == 0 else (slice(2, 4), 0)
            return ps[:, banks, at:at + 2 * RC].rearrange("p a (k c) -> p a k c", k=2)

        def chunk(k, c):
            return k * FULL + c if c < FULL else UT * FULL + k // 2

        def tiles_of_chunk(e):
            return [(k, c) for k in range(UT) for c in range(CH) if chunk(k, c) == e]

        def group_of(tensor, g):
            return tensor[:, bass.ds(g * UT, UT), :]

        @block.sync
        def _(sp):
            sp.dma_start(x[:, :, :], x_in.rearrange("(t p) c -> p t c", p=P)).then_inc(x_loaded, 16)
            sp.dma_start(w[0:C + 1, :], blob_in).then_inc(w_loaded, 16)

            def tiles_of(dram, g):
                return dram.rearrange("(t p) c -> t p c", p=P)[bass.ds(g * UT, UT), :, :].rearrange("t p c -> p t c")

            def store_table(n, g):
                sp.wait_ge(table_ready, g + (LAYER_OF[n] * NGR + 1))
                sp.dma_start(tiles_of(tables[LAYER_OF[n] % 2], g), group_of(tab, g)).then_inc(table_stored, 16)

            def store_result(g):
                sp.wait_ge(nodes_ready, unit_no(6, g) + (1 - NGR))
                sp.dma_start(tiles_of(out, g), group_of(x, g)).then_inc(out_stored, 16)

            def build_load(t, first):
                for r in range(NQ):
                    if not first:
                        sp.wait_ge(converted, t * NQ + (r + 1 - NQ))
                    sp.dma_start(adjq[:, r, :], adj_t[bass.ds(t, 1), :, r * QC:(r + 1) * QC].rearrange(
                        "a p j -> p (a j)")).then_inc(conv_loaded[r], 16)
            for t in range(UT):
                build_load(t, t == 0)
            with sp.Fori(0, NGR - 1) as g:
                for k in range(UT):
                    build_load(g * UT + (UT + k), False)
                store_table(0, g)
            store_table(0, NGR - 1)

            sp.wait_ge(flag_ready, 1)
            dense = sp.value_load(flag[0:1, 0:1])
            with sp.If(dense):
                for l in range(NL):
                    def load(t, first):
                        for h in range(NQ):
                            if not first:
                                sp.wait_ge(adj_used, t * NQ + (l * NT * NQ + h + 1 - NQ))
                            sp.dma_start(adjq[:, h, :], adj_t[bass.ds(t, 1), :, h * QC:(h + 1) * QC].rearrange(
                                "a p j -> p (a j)")).then_inc(adj_loaded[h], 16)
                    load(0, l == 0)
                    with sp.Fori(1, NT) as t:
                        load(t, False)
                with sp.Fori(0, NGR) as g:
                    store_result(g)
            with sp.Else():
                for n in (1, 3, 4, 5):
                    with sp.Fori(0, NGR) as g:
                        store_table(n, g)
                with sp.Fori(0, NGR) as g:
                    store_result(g)
                sp.wait_ge(table_stored, NL * NGR * 16)
            sp.wait_ge(out_stored, NGR * 16)

        @block.gpsimd
        def _(pool):
            pool.memset(ident[:, :], 0.0).then_inc(const_made, 1)
            pool.memset(ones, 1.0).then_inc(const_made, 1)
            pool.memset(tab[:, :, C + 1:C + 2], 1.0).then_inc(const_made, 1)
            pool.wait_ge(const_made, 3)
            pool.memset(xt[C:C + 1, :, :], 1.0).then_inc(const_made, 1)
            pool.wait_ge(const_made, 4)
            pool.affine_select(out=ident[:, :], in_=ident[:, :], compare_op=ALU.not_equal, fill=1.0,
                               base=0, pattern=[[-1, P]], channel_multiplier=1).then_inc(const_made, 1)
            for a in range(2):
                pool.iota(number[:, a, 0:FULL * P], [[1, FULL * P]], base=0, channel_multiplier=0,
                          allow_small_or_imprecise_dtypes=True).then_inc(sparse_const, 1)
                h = FULL * P + a * P // 2
                pool.iota(number[:, a, h:h + P // 2], [[1, P // 2]], base=FULL * P, channel_multiplier=0,
                          allow_small_or_imprecise_dtypes=True).then_inc(sparse_const, 1)
                h = FULL * P + (1 - a) * P // 2
                pool.memset(number[:, a, h:h + P // 2], -1.0).then_inc(sparse_const, 1)
            pool.iota(gnum[:, 0, :], [[GLOW, GW // GLOW], [0, GLOW]], base=0, channel_multiplier=0,
                      allow_small_or_imprecise_dtypes=True).then_inc(sparse_const, 1)
            pool.iota(gnum[:, 1, :], [[0, GW // GLOW], [1, GLOW]], base=0, channel_multiplier=0,
                      allow_small_or_imprecise_dtypes=True).then_inc(sparse_const, 1)
            pool.memset(oneb, 1.0).then_inc(sparse_const, 1)
            pool.iota(posc[:, 0:UT * FULL].rearrange("p (k c) -> p k c", k=UT), [[0, UT], [P, FULL]], base=0,
                      channel_multiplier=1,
                      allow_small_or_imprecise_dtypes=True).then_inc(sparse_const, 1)
            pool.iota(posc[:, UT * FULL:NE], [[0, UT // 2]], base=FULL * P, channel_multiplier=1,
                      allow_small_or_imprecise_dtypes=True).then_inc(sparse_const, 1)
            pool.iota(lst[:, :, SLOTS + 1], [[0, UT]], base=1, channel_multiplier=1,
                      allow_small_or_imprecise_dtypes=True).then_inc(sparse_const, 1)
            pool.iota(iotab, [[1, P]], base=0, channel_multiplier=0,
                      allow_small_or_imprecise_dtypes=True).then_inc(sparse_const, 1)
            pool.memset(identb, 0.0).then_inc(sparse_const, 1)
            pool.memset(sid, 0.0).then_inc(sparse_const, 1)
            pool.memset(below, 1.0).then_inc(sparse_const, 1)
            pool.wait_ge(sparse_const, FILLED)
            pool.affine_select(out=identb, in_=identb, compare_op=ALU.not_equal, fill=1.0,
                               base=0, pattern=[[-1, P]], channel_multiplier=1).then_inc(sparse_const, 1)
            for b in range(GB):
                pool.affine_select(out=sid[:, b, :], in_=sid[:, b, :], compare_op=ALU.not_equal, fill=float(GW << b),
                                   base=0, pattern=[[-1, P]], channel_multiplier=1).then_inc(sparse_const, 1)
            pool.affine_select(out=below, in_=below, compare_op=ALU.is_gt, fill=0.0,
                               base=0, pattern=[[1, P]], channel_multiplier=-1).then_inc(sparse_const, 1)

            def gather(l, g, i, b, first):
                if not first:
                    pool.wait_ge(gathered[b], i * (16 * NE) + l * (NGR // 2) * 16 * NE)
                    if SLOPE[l] is None:
                        pool.wait_ge(sum_mm, g + (l * NGR - 1))
                    else:
                        pool.wait_ge(fs_ready, g + (gats_before(l) * NGR - 1))
                pool.tensor_copy(ixs[:, b, :], idx[:, bass.ds(g * NE, NE)]).then_inc(idx_staged, 1)
                pool.wait_ge(idx_staged, g + (l * NGR + 1))
                pool.sem_inc(waited_pool, 1)
                for e in range(NE):
                    pool.indirect_dma_start(feat[:, b, e, :], None, tables[l % 2],
                                            bass.IndirectOffsetOnAxis(ap=ixs[:, b, e:e + 1], axis=0)).then_inc(gathered[b], 16)

            pool.wait_ge(table_stored, 16 * NGR)
            pool.wait_ge(lists_ready, 2)
            gather(0, 0, 0, 0, True)
            gather(0, 1, 0, 1, True)
            pool.wait_ge(flag_ready, 1)
            dense = pool.value_load(flag[0:1, 0:1])
            for l in range(NL):
                with pool.If(dense):
                    pool.nop()
                with pool.Else():
                    if l == 0:
                        pool.wait_ge(lists_ready, NGR)
                    else:
                        pool.wait_ge(table_stored, 16 * NGR * (l + 1))
                        pool.wait_ge(sum_mm, l * NGR)
                        gather(l, 0, 0, 0, True)
                        gather(l, 1, 0, 1, True)
                    with pool.Fori(1, NGR // 2) as i:
                        for b in range(2):
                            gather(l, 2 * i + b, i, b, False)

        @block.tensor
        def _(pe):
            pe.wait_ge(w_loaded, 16)
            pe.wait_ge(const_made, 5)
            for l in range(2):
                for k in range(2):
                    mm = pe.matmul(ps[0:C, 0, 2 * l + k:2 * l + k + 1], w[0:HID, LT + (2 * l + k) * C:LT + (2 * l + k + 1) * C],
                                   w[0:HID, AV + l:AV + l + 1], start=True, stop=True)
            mm.then_inc(w_mm, 1)
            pe.wait_ge(w_cp, 1)
            for l in GATS:
                o = ps[0:C + 1, 1 + WT_OF[l], 0:2]
                rhs = a2[:, l, :] if l < 2 else w[0:C, A2 + 2 * (l - 3):A2 + 2 * (l - 2)]
                lhs = w[0:C, WT + WT_OF[l] * (C + 1):WT + (WT_OF[l] + 1) * (C + 1)]
                mm = pe.matmul(o, lhs, rhs, start=True, stop=(l >= 2))
                if l < 2:
                    mm = pe.matmul(ps[0:C + 1, 1 + WT_OF[l], 1:2], w[0:HID, LB + l * (C + 1):LB + (l + 1) * (C + 1)],
                                   w[0:HID, AV + l:AV + l + 1], start=False, stop=True)
            mm.then_inc(w_mm, 1)
            pe.wait_ge(w_cp, 2)

            def turn(n, g, b):
                u = unit_no(n, g)
                pe.wait_ge(staged, u + 1)
                if not (isinstance(u, int) and u == 0):
                    pe.wait_ge(xt_copied, u)
                for k in range(UT):
                    mm = pe.matmul(ps[0:C, 7, k * P:(k + 1) * P], stage[:, buffer_of(n, b), k, :], ident[:, :],
                                   start=True, stop=True)
                mm.then_inc(t_turned, 1)

            def product(n, g, b):
                u = unit_no(n, g)
                pe.wait_ge(xt_copied, u + 1)
                if not (isinstance(u, int) and u == 0):
                    pe.wait_ge(proj_used, u - 1 if n in (2, 3) else u)
                l = LAYER_OF[n]
                rhs = w[0:C + 1, MLP2:MLP2 + C] if l is None else w[0:C + 1, l * RC:(l + 1) * RC]
                for k in range(UT):
                    if l is None:
                        o = ps[:, 4, SECOND + k * C:SECOND + (k + 1) * C]
                    else:
                        o = product_of(n)[:, k // 2, k % 2, :]
                    mm = pe.matmul(o,
                                   xt[:, buffer_of(n, b), k * P:(k + 1) * P], rhs, start=True, stop=True)
                mm.then_inc(proj_done, 1)

            def spread(l):
                base = gats_before(l) * NU
                pe.wait_ge(ones_made, gats_before(l) + 1)

                def unit(q, b, first):
                    pe.wait_ge(diag_made, q + (base + 1))
                    if not first:
                        pe.wait_ge(vb_ready, q + (base - 1))
                    pe.matmul(ps[:, b, :], s[:, 0, 0:P], pt[:, b, :], start=True, stop=True).then_inc(vb_summed, 1)
                unit(0, 0, l == 0)
                unit(1, 1, l == 0)
                with pe.Fori(1, NU // 2) as i:
                    for b in range(2):
                        unit(2 * i + b, b, False)
                pe.wait_ge(vb_ready, base + NU)

            def aggregate(l):
                if SLOPE[l] is not None:
                    spread(l)

                def tile(t, b, first):
                    if SLOPE[l] is None:
                        pe.wait_ge(m_ready, t + 1)
                    else:
                        pe.wait_ge(p_ready, t + (gats_before(l) * NT + 1))
                    tb = t * NB + l * NT * NB

                    def turned(g):
                        if not (first and g < 2):
                            pe.wait_ge(pt_copied, tb + (g - 1))
                        for k in range(TB):
                            j = g * TB + k
                            mm = pe.transpose(ps[:, g % 2, k * P:(k + 1) * P], s[:, b, j * P:(j + 1) * P], ident[:, :])
                        mm.then_inc(p_turned, 1)

                    def summed(g):
                        pe.wait_ge(pt_copied, tb + (g + 1))
                        for k in range(TB):
                            j = g * TB + k
                            mm = pe.matmul(ps[:, 2 + b, 0:TC], pt[:, g % 2, k * P:(k + 1) * P], tab[:, j, 0:TC],
                                           start=(j == 0), stop=(j == NT - 1))
                        mm.then_inc(pt_used, 1)

                    turned(0)
                    if not (l == 0 and isinstance(t, int) and t < 2):
                        pe.wait_ge(agg_used, t + (l * NT - 1))
                    for g in range(NB):
                        if g + 1 < NB:
                            turned(g + 1)
                        summed(g)

                tile(0, 0, l == 0)
                tile(1, 1, False)
                with pe.Fori(1, NT // 2) as i:
                    for b in range(2):
                        tile(2 * i + b, b, False)

            def fold(t, b):
                pe.wait_ge(diag_cut, t + 1)
                if not (isinstance(t, int) and t < 2):
                    pe.wait_ge(code_used, t - 1)
                for h in range(2):
                    for r in range(2):
                        pe.matmul(ps[:, 2 * b + h, :], oneb[0:1, :], gnum[0:1, r, h * 512:(h + 1) * 512],
                                  start=(r == 0), stop=False)
                for k in range(GB):
                    for h in range(2):
                        mm = pe.matmul(ps[:, 2 * b + h, :], sid[:, k, :], ab[:, b, k * GW + h * 512:k * GW + (h + 1) * 512],
                                       start=False, stop=(k == GB - 1))
                mm.then_inc(folded, 1)

            def lists(g, first):
                pe.wait_ge(deg_ready, g + 1)
                if not first:
                    pe.wait_ge(lists_ready, g)
                pe.matmul(ps[:, 4, 0:UT], below, deg4, start=True, stop=True).then_inc(base_mm, 1)
                for k in range(UT):
                    pe.wait_ge(mf_ready, g * UT + (k + 1))
                    for c in range(FULL):
                        e = k * FULL + c
                        for r in range(2):
                            mm = pe.matmul(ps[:, 5, e * LW:(e + 1) * LW], mf[:, k % 2, c * P:(c + 1) * P], lstb[:, r, k, :],
                                           start=(r == 0), stop=(r == 1))
                    if k % 2 == 1:
                        e = UT * FULL + k // 2
                        for j in range(4):
                            mm = pe.matmul(ps[:, 5, e * LW:(e + 1) * LW], mf[:, j // 2, FULL * P:CH * P],
                                           lstb[:, j % 2, k - 1 + j // 2, :], start=(j == 0), stop=(j == 3))
                    mm.then_inc(list_mm, 1)

            def build_group(g, first, last):
                for k in range(UT):
                    if not (last and k == UT - 1):
                        fold(g * UT + (k + 1), (k + 1) % 2)
                    if k == 0:
                        turn(0, g, 0)
                    if k == 1:
                        product(0, g, 0)
                lists(g, first)

            def sparse(l):
                gat = SLOPE[l] is not None
                banks = [0, 1]

                def turned_rows(g, b):
                    pe.wait_ge(st_ready, g + (l * NGR + 1))
                    for c in range(CH):
                        m = g * CH + (gats_before(l) * NGR * CH + c)
                        if not (isinstance(m, int) and m < len(banks)):
                            pe.wait_ge(mb_copied, m + (1 - len(banks)))
                        for k in range(UT):
                            mm = pe.matmul(ps[:, banks[c % len(banks)], k * P:(k + 1) * P],
                                           st[:, b, c * UT + k, :], identb, start=True, stop=True)
                        mm.then_inc(mt_turned, 1)

                def turn_of(g, i, b):
                    if gat and has(g):
                        gn = g + (gats_before(l) * NGR + 1)
                        pe.wait_ge(q_ready, gn)
                        for k in range(UT):
                            for c in range(CH):
                                mm = pe.matmul(ps[:, 4, k * SLOTS * 3:(k + 1) * SLOTS * 3], st[:, b, k * CH + c, :],
                                               qv[:, chunk(k, c), :, :].rearrange("p s r -> p (s r)"),
                                               start=(c == 0), stop=(c == CH - 1))
                        mm.then_inc(vp_mm, 1)
                    if l == 1 and has(g - 3):
                        turn(3, g - 3, 1 - b)
                    if gat and has(g):
                        turned_rows(g, b)
                    if l < NL - 1 and has(g - 2):
                        turn(AFTER[l][0], g - 2, b)
                    if gat and has(g):
                        pe.wait_ge(mb_copied, g * CH + (gats_before(l) * NGR + 1) * CH)
                        pe.wait_ge(um_ready, gn)
                        for e in range(NE):
                            tiles = tiles_of_chunk(e)
                            for k, c in tiles:
                                mm = pe.matmul(ps[:, 5, e * 6:(e + 1) * 6], mb[:, (k * CH + c) * P:(k * CH + c + 1) * P],
                                               um[:, k, :, :].rearrange("p a r -> p (a r)"),
                                               start=((k, c) == tiles[0]), stop=((k, c) == tiles[-1]))
                        mm.then_inc(um_mm, 1)
                    if l == 1 and has(g - 3):
                        product(3, g - 3, 1 - b)
                    if l < NL - 1 and has(g - 2):
                        product(AFTER[l][0], g - 2, b)
                    if has(g):
                        pe.wait_ge(stf_ready, g * 2 + (l * NGR + 1) * 2)
                        if gat:
                            pe.wait_ge(fs_ready, gn)
                        else:
                            pe.wait_ge(gathered[b], i * (16 * NE) + (l * (NGR // 2) + 1) * 16 * NE)
                        if not gat and has(g - 1):
                            pe.wait_ge(sum_used, g + sum(k < l for k in range(NL) if k not in ELUS) * NGR)
                        for k in range(UT):
                            for c in range(CH):
                                e = chunk(k, c)
                                mm = pe.matmul(ps[:, 6, k * TC:(k + 1) * TC], stf[:, k * CH + c, :],
                                               fs[:, e, :] if gat else feat[:, b, e, 0:TC],
                                               start=(c == 0), stop=(c == CH - 1))
                            if k == UT // 2 - 1:
                                mm.then_inc(half_sum_mm, 1)
                        mm.then_inc(sum_mm, 1)
                pipelined(pe, turn_of, PE_LAG[l])

            pe.wait_ge(sparse_const, SPARSE_CONSTS)
            fold(0, 0)
            build_group(0, True, False)
            with pe.Fori(1, NGR - 1) as g:
                build_group(g, False, False)
            build_group(NGR - 1, False, True)
            pe.wait_ge(bad_ready, 1)
            pe.matmul(ps[:, 4, 0:1], ones, badn, start=True, stop=True).then_inc(bad_mm, 1)
            pe.wait_ge(flag_ready, 1)
            dense = pe.value_load(flag[0:1, 0:1])
            for l in range(NL):
                with pe.If(dense):
                    aggregate(l)
                    if l < NL - 1:
                        with pe.Fori(0, NGR // 2) as i:
                            for b in range(2):
                                for n in AFTER[l]:
                                    turn(n, 2 * i + b, b)
                                    product(n, 2 * i + b, b)
                    else:
                        pe.nop()
                with pe.Else():
                    sparse(l)

        @block.scalar
        def _(act):
            def put(n, g, b, near=False):
                u = unit_no(n, g)
                if n > 0:
                    act.wait_ge(nodes_ready, u + (1 - NGR))
                if near:
                    if not (isinstance(u, int) and u == 0):
                        act.wait_ge(t_turned, u)
                elif not (isinstance(u, int) and u < 2):
                    act.wait_ge(t_turned, u - 1)
                act.activation(stage[:, buffer_of(n, b), :, :], group_of(hid if n in (1, 2) else x, g),
                               ACT.Copy).then_inc(staged, 1)

            def take_turned(n, g, b, near=False):
                u = unit_no(n, g)
                act.wait_ge(t_turned, u + 1)
                if near:
                    if not (isinstance(u, int) and u == 0):
                        act.wait_ge(proj_done, u)
                elif not (isinstance(u, int) and u < 2):
                    act.wait_ge(proj_done, u - 1)
                act.activation(xt[0:C, buffer_of(n, b), :], ps[0:C, 7, :], ACT.Copy).then_inc(xt_copied, 1)

            def elu_exp_of(l, g):
                act.wait_ge(elu_in, elu_no(l, g) + 1)
                act.activation(eb, eb, ACT.Exp).then_inc(elu_exp, 1)

            def aggregate(l):
                gat = SLOPE[l] is not None
                gb = gats_before(l) * NT
                if gat:
                    base = gats_before(l) * NU
                    with act.Fori(0, NU // 2) as i:
                        for b in range(2):
                            act.wait_ge(vb_summed, 2 * i + (base + b + 1))
                            act.activation(vb[:, bass.ds((2 * i + b) * UT * P, UT * P)], ps[:, b, :], ACT.Copy).then_inc(vb_ready, 1)
                    act.wait_ge(vb_ready, base + NU)

                def scores(t, b, first):
                    if not first:
                        act.wait_ge(pt_used, (t + (l * NT - 1)) * NB)
                    act.activation(s[:, b, :], vb[:, :], ACT.Identity, bias=own[:, bass.ds(t, 1)]).then_inc(z_ready, 1)

                def tile(t, b, first):
                    if gat:
                        act.wait_ge(max_ready, t + (gb + 1))
                        act.activation(s[:, b, :], s[:, b, :], ACT.Exp, bias=nmax[:, b:b + 1]).then_inc(p_ready, 1)
                    tb = t * NB + l * NT * NB
                    for g in range(NB):
                        act.wait_ge(p_turned, tb + (g + 1))
                        if not (first and g < 2):
                            act.wait_ge(pt_used, tb + (g - 1))
                        act.activation(pt[:, g % 2, :], ps[:, g % 2, :], ACT.Copy).then_inc(pt_copied, 1)

                if gat:
                    scores(0, 0, True)
                    scores(1, 1, True)
                tile(0, 0, l == 0)
                if gat:
                    scores(2, 0, False)
                tile(1, 1, False)
                with act.Fori(1, NT // 2 - 1) as i:
                    for b in range(2):
                        if gat:
                            scores(2 * i + (b + 1), 1 - b, False)
                        tile(2 * i + b, b, False)
                if gat:
                    scores(NT - 1, 1, False)
                tile(NT - 2, 0, False)
                tile(NT - 1, 1, False)

            def convert(t, b, first):
                for r in range(NQ):
                    act.wait_ge(conv_loaded[r], t * 16 + 16)
                    if r == 0 and not first:
                        act.wait_ge(folded, t - 1)
                    act.activation(ab[:, b, r * QC:(r + 1) * QC], adjq[:, r, :], ACT.Copy,
                                   accum_out=rs[:, bass.ds(t, 1), r]).then_inc(converted, 1)

            def sparse(l):
                gat = SLOPE[l] is not None
                gb = gats_before(l) * NGR
                banks = [0, 1]

                def copy_rows(g):
                    for c in range(CH):
                        act.wait_ge(mt_turned, g * CH + (gb * CH + c + 1))
                        act.activation(mb[:, c * UT * P:(c + 1) * UT * P], ps[:, banks[c % len(banks)], :],
                                       ACT.Copy).then_inc(mb_copied, 1)

                def rows_in_float32(g, b, half):
                    es = slice(half * UT * CH // 2, (half + 1) * UT * CH // 2)
                    act.wait_ge(st_ready, g + (l * NGR + 1))
                    if not (l == 0 and isinstance(g, int) and g == 0):
                        act.wait_ge(sum_mm if half else half_sum_mm, g + l * NGR)
                    act.activation(stf[:, es, :], st[:, b, es, :], ACT.Copy).then_inc(stf_ready, 1)

                def turn_of(g, i, b):
                    if l == 1 and has(g - 3):
                        put(3, g - 3, 1 - b)
                    if l < NL - 1 and has(g - 2):
                        put(AFTER[l][0], g - 2, b)
                    if l == 1 and has(g - 3):
                        take_turned(3, g - 3, 1 - b)
                    if gat and has(g):
                        copy_rows(g)
                    if l < NL - 1 and has(g - 2):
                        take_turned(AFTER[l][0], g - 2, b)
                    if has(g):
                        rows_in_float32(g, b, 1)
                    if gat and has(g):
                        act.wait_ge(self_in, g + (gb + 1))
                        act.activation(ws, ws, ACT.Exp).then_inc(self_exp, 1)
                        act.wait_ge(edge_in, g + (gb + 1))
                        act.activation(we, we, ACT.Exp).then_inc(edge_exp, 1)
                    if l in ELUS and has(g - 1):
                        elu_exp_of(l, g - 1)
                    if has(g + 1):
                        rows_in_float32(g + 1, 1 - b, 0)

                rows_in_float32(0, 0, 0)
                pipelined(act, turn_of, ACT_LAG[l])

            act.wait_ge(x_loaded, 16)
            convert(0, 0, True)
            convert(1, 1, True)

            def build_group(g, last):
                put(0, g, 0, True)
                for k in range(UT):
                    if not (last and k >= UT - 2):
                        convert(g * UT + (k + 2), k % 2, False)
                    if k == 0:
                        take_turned(0, g, 0, True)
            build_group(0, False)
            with act.Fori(1, NGR - 1) as g:
                build_group(g, False)
            build_group(NGR - 1, True)
            act.wait_ge(flag_ready, 1)
            dense = act.value_load(flag[0:1, 0:1])
            for l in range(NL):
                with act.If(dense):
                    aggregate(l)
                    with act.Fori(0, NGR // 2) as i:
                        for b in range(2):
                            if l in ELUS:
                                elu_exp_of(l, 2 * i + b)
                            if l < NL - 1:
                                for n in AFTER[l]:
                                    put(n, 2 * i + b, b)
                                    take_turned(n, 2 * i + b, b)
                            elif l not in ELUS:
                                act.nop()
                with act.Else():
                    sparse(l)

        @block.vector
        def _(dve):
            dense_count = Count(dense_step)
            build_count = Count(build_step)
            sparse_count = Count(sparse_step)
            epi_count = Count(epi_step)
            score_count = Count(score_step)
            post_count = Count(vec_step)
            second_count = Count(second_step)

            def link(ins, count, between=None):
                ins.then_inc(count.sem, 1)
                count.k += 1
                if between is not None:
                    between()
                dve.wait_ge(count.sem, count.at())

            def dlink(ins):
                link(ins, dense_count)

            def blink(ins):
                link(ins, build_count)

            class Between:
                fill = None

            def slink(ins, between=None):
                link(ins, sparse_count, between or Between.fill)

            def elink(ins):
                link(ins, epi_count)

            dve.wait_ge(w_loaded, 16)
            dve.wait_ge(w_mm, 1)
            dve.tensor_copy(a2[:, :, :], ps[0:C, 0, 0:4].rearrange("p (l k) -> p l k", l=2)).then_inc(w_cp, 1)
            dve.wait_ge(w_mm, 2)
            for l in GATS:
                cp = dve.tensor_copy(w[0:C + 1, l * RC + C:l * RC + TC], ps[0:C + 1, 1 + WT_OF[l], 0:2])
            cp.then_inc(w_cp, 1)
            dve.wait_ge(const_made, 5)

            def take_products(n, g, stored=False, between=None):
                l = LAYER_OF[n]
                if stored and l > 0:
                    dve.wait_ge(table_stored, 16 * NGR * l)
                dve.wait_ge(proj_done, unit_no(n, g) + 1)
                halves = [group_of(v, g).rearrange("p (a k) c -> p a k c", k=2) for v in (res, x, tab)]
                both = product_of(n)
                if l is None:
                    dve.tensor_tensor(group_of(res, g), ps[:, 4, SECOND:SECOND + UT * C].rearrange("p (k c) -> p k c", c=C),
                                      group_of(res, g), ALU.add).then_inc(proj_used, 1)
                    dve.wait_ge(proj_used, unit_no(n, g) + 1)
                    return
                dve.tensor_tensor(halves[0], both[:, :, :, TC:RC], halves[0 if n == 1 else 1], ALU.add)
                score_count.start(l * NGR * 3, g, 3)
                clink = lambda ins: link(ins, score_count, between)
                dve.tensor_copy(halves[2][:, :, :, 0:C + 1], both[:, :, :, 0:C + 1])
                dve.tensor_copy(own[:, bass.ds(g * UT, UT)].rearrange("p (a k) -> p a k", k=2),
                                both[:, :, :, C + 1]).then_inc(proj_used, 1)
                dve.wait_ge(proj_used, unit_no(n, g) + 1)
                v, hi, mid, lo = (tab[:, bass.ds(g * UT, UT), c] for c in (C, C + 2, C + 3, C + 4))
                top = lambda o, a: dve.tensor_scalar(o.bitcast(I32), a.bitcast(I32), 16, 16, ALU.logical_shift_right,
                                                     ALU.logical_shift_left)
                clink(top(hi, v))
                clink(dve.tensor_tensor(lo, v, hi, ALU.subtract))
                clink(top(mid, lo))
                dve.tensor_tensor(lo, lo, mid, ALU.subtract).then_inc(table_ready, 1)

            def aggregate(l):
                gat = SLOPE[l] is not None
                if gat:
                    base = gats_before(l) * NU

                    def diagonals(q, b, first):
                        if not first:
                            dve.wait_ge(vb_summed, q + (base - 1))
                        for k in range(UT):
                            d = dve.tensor_scalar(pt[:, b, k * P:(k + 1) * P], ident[:, :],
                                                  tab[:, bass.ds(q * UT + k, 1), C:C + 1].rearrange(
                                                      "p a c -> p (a c)"), None, ALU.mult)
                        d.then_inc(diag_made, 1)
                    dve.memset(s[:, 0, 0:P], 1.0).then_inc(ones_made, 1)
                    diagonals(0, 0, l == 0)
                    diagonals(1, 1, l == 0)
                    with dve.Fori(1, NU // 2) as i:
                        for b in range(2):
                            diagonals(2 * i + b, b, False)

                def edges(t, b):
                    if gat:
                        dve.wait_ge(z_ready, t + (gats_before(l) * NT + 1))
                        dlink(dve.scalar_tensor_tensor(out=s[:, b, :], in0=s[:, b, :], scalar=SLOPE[l], in1=s[:, b, :],
                                                      op0=ALU.mult, op1=ALU.max))
                    elif not (isinstance(t, int) and t < 2):
                        dve.wait_ge(pt_used, (t + (l * NT - 1)) * NB)
                    for h in range(NQ):
                        dve.wait_ge(adj_loaded[h], t * 16 + (l * NT + 1) * 16)
                        sh = s[:, b, h * QC:(h + 1) * QC]
                        if gat:
                            m = adjq[:, h, :].bitcast(F32)
                            dlink(dve.tensor_scalar(m, adjq[:, h, :], 0, NEG, ALU.is_gt, ALU.mult))
                            dve.scalar_tensor_tensor(out=sh, in0=m, scalar=-NEG, in1=sh,
                                                     op0=ALU.add, op1=ALU.add).then_inc(adj_used, 1)
                        else:
                            dve.tensor_scalar(sh, adjq[:, h, :], 1, None, ALU.is_equal).then_inc(adj_used, 1)
                    dve.wait_ge(adj_used, t * NQ + (l * NT * NQ + NQ))
                    if gat:
                        dve.tensor_reduce(nmax[:, b:b + 1], s[:, b, :], AX, ALU.max, negate=True).then_inc(max_ready, 1)
                    else:
                        dve.tensor_copy(nmax[:, b:b + 1], ident[:, 0:1]).then_inc(m_ready, 1)

                def divided(t, b):
                    dve.wait_ge(pt_used, (t + (l * NT + 1)) * NB)
                    dlink(dve.reciprocal(rden[:, b:b + 1], ps[:, 2 + b, C + 1:TC]))
                    dve.tensor_scalar(hid[:, bass.ds(t, 1), :].rearrange("p a c -> p (a c)"), ps[:, 2 + b, 0:C],
                                      rden[:, b:b + 1], None, ALU.mult).then_inc(agg_used, 1)

                base = gats_before(l) * NT * (2 + NQ) + (l - gats_before(l)) * NT
                per = 2 + NQ if gat else 1
                dense_count.start(base, 0, per - 1)
                edges(0, 0)
                dense_count.start(base - 1, 1, per)
                edges(1, 1)
                divided(0, 0)
                with dve.Fori(1, NT // 2) as i:
                    for b in range(2):
                        dense_count.start(base - 1, 2 * i + b, per)
                        edges(2 * i + b, b)
                        divided(2 * i + (b - 1), 1 - b)
                dense_count.start(base + NT * per - 1, 0, 1)
                divided(NT - 1, 1)
                dve.wait_ge(agg_used, (l + 1) * NT)

            def cut_diagonal(t, b):
                dve.wait_ge(converted, t * NQ + NQ)
                if not (isinstance(t, int) and t == 0):
                    dve.wait_ge(diag_cut, t)
                blk = ab[:, b, bass.ds(t * P, P)]
                blink(dve.scalar_tensor_tensor(out=dtmp, in0=blk, scalar=1.0, in1=identb, op0=ALU.mult, op1=ALU.mult,
                                               accum_out=dg[:, bass.ds(t, 1)]))
                dve.tensor_tensor(blk, blk, dtmp, ALU.subtract).then_inc(diag_cut, 1)

            BUILD = UT * (1 + 1) + 19

            def settled():
                dve.sem_inc(waited_vec, 1)

            def code_keys(t, k, b):
                dve.wait_ge(folded, t + 1)
                if not (isinstance(t, int) and t == 0):
                    dve.wait_ge(keys_ready, t)
                key = ps[:, 2 * b:2 * b + 2, :].rearrange("p h g -> p (h g)")
                settled()
                blink(dve.max(keys[:, k, 0:8], key))
                settled()
                dve.match_replace(keyb, keys[:, k, 0:8], key, 0.0).then_inc(code_used, 1)
                dve.wait_ge(code_used, t + 1)
                settled()
                dve.max(keys[:, k, 8:16], keyb).then_inc(keys_ready, 1)

            def build_lists(g):
                n = bass.ds(g * UT, UT)
                ne = bass.ds(g * NE, NE)
                dve.wait_ge(keys_ready, g * UT + UT)
                blink(dve.tensor_copy(ki, keys.rearrange("p k s -> p (k s)")))
                dve.tensor_scalar(gi, ki, 0, GW - 1, ALU.logical_shift_right, ALU.bitwise_and)
                for b in range(GB):
                    bit = dve.tensor_scalar(bits[:, b, :], ki, LOG_GW + b, 1, ALU.logical_shift_right, ALU.bitwise_and)
                blink(bit)
                for b in range(GB):
                    c = dve.scalar_tensor_tensor(out=cand[:, :, b, :], in0=gi.rearrange("p (k s) -> p k s", k=UT),
                                                 scalar=float(GW * b + 1), in1=bits[:, b, :].rearrange("p (k s) -> p k s", k=UT),
                                                 op0=ALU.add, op1=ALU.mult)
                blink(c)
                settled()
                flat = [cand[:, k, :, :].rearrange("p b s -> p (b s)") for k in range(UT)]
                for k in range(UT):
                    m = dve.max(lst[:, k, 0:8], flat[k])
                blink(m)
                settled()
                for k in range(UT):
                    m = dve.match_replace(flat[k], lst[:, k, 0:8], flat[k], 0.0)
                blink(m)
                settled()
                for k in range(UT):
                    m = dve.max(lst[:, k, 8:16], flat[k])
                blink(m)
                blink(dve.tensor_scalar(valid, lst[:, :, 0:SLOTS], 0.0, None, ALU.is_gt))
                dve.tensor_scalar(vbias[:, n, :], valid, -1.0, BIG, ALU.add, ALU.mult)
                dve.tensor_reduce(deg4, valid, AX, ALU.add).then_inc(deg_ready, 1)
                dve.wait_ge(base_mm, g + 1)
                base = ps[:, 4, 0:UT]
                dve.tensor_copy(lst[:, :, SLOTS], base)
                dve.tensor_copy(deg[:, n], deg4)
                dve.tensor_tensor(endall[:, n], base, deg4, ALU.add)
                blink(dve.tensor_tensor(end4, base, deg4, ALU.add))
                blink(dve.tensor_copy(lstb[:, 0, :, :], lst))
                blink(dve.tensor_tensor(lstb[:, 1, :, :], lst, lstb[:, 0, :, :], ALU.subtract))
                for k in range(UT):
                    if k > 0:
                        dve.wait_ge(mf_ready, g * UT + k)
                    blink(dve.tensor_scalar(mtmp, number[:, k % 2, :], lst[:, k, SLOTS:SLOTS + 1], None, ALU.is_ge))
                    if k >= 2:
                        dve.wait_ge(list_mm, g * UT + (k - k % 2))
                    dve.scalar_tensor_tensor(out=mf[:, k % 2, :], in0=number[:, k % 2, :], scalar=end4[:, k:k + 1], in1=mtmp,
                                             op0=ALU.is_lt, op1=ALU.mult).then_inc(mf_ready, 1)
                dve.wait_ge(list_mm, g * UT + UT)
                rows = ps[:, 5, 0:NE * LW].rearrange("p (e s) -> p e s", s=LW)
                dve.tensor_scalar(rowi[:, n, 0:FULL], rows[:, 0:UT * FULL, SLOTS + 1].rearrange("p (k c) -> p k c", k=UT),
                                  -1.0, None, ALU.add)
                for a in range(2):
                    dve.tensor_scalar(rowi[:, n, FULL].rearrange("p (j a) -> p j a", a=2)[:, :, a], rows[:, UT * FULL:NE, SLOTS + 1],
                                      whose[:, a:a + 1], -1.0, ALU.mult, ALU.add)
                blink(dve.tensor_tensor(slot[:, ne], posc, rows[:, :, SLOTS], ALU.subtract))
                all3 = [P, NE, SLOTS]
                blink(dve.tensor_tensor(oh, iota[:, 0:SLOTS].unsqueeze(1).to_broadcast(all3),
                                        slot[:, ne].unsqueeze(2).to_broadcast(all3), ALU.is_equal))
                blink(dve.tensor_tensor(oh, oh, rows[:, :, 0:SLOTS], ALU.mult))
                blink(dve.tensor_reduce(idx1, oh, AX, ALU.add))
                blink(dve.tensor_scalar(idx1, idx1, 1.0, float(N), ALU.max, ALU.min))
                dve.tensor_scalar(idx[:, ne], idx1, -1.0, None, ALU.add).then_inc(lists_ready, 1)

            def judged():
                dve.wait_ge(lists_ready, NGR)
                build_count.start(NGR * BUILD, 0, 4)
                dve.tensor_reduce(rsum, rs, AX, ALU.add)
                blink(dve.tensor_tensor(tot, deg, dg, ALU.add))
                blink(dve.tensor_tensor(bad, tot, rsum, ALU.not_equal))
                blink(dve.scalar_tensor_tensor(out=bad, in0=tot, scalar=1.0, in1=bad, op0=ALU.is_lt, op1=ALU.add))
                blink(dve.scalar_tensor_tensor(out=bad, in0=endall, scalar=float(CAP), in1=bad, op0=ALU.is_gt, op1=ALU.add))
                dve.tensor_scalar(dgb, dg, -1.0, BIG, ALU.add, ALU.mult)
                dve.tensor_reduce(badn, bad, AX, ALU.add).then_inc(bad_ready, 1)
                dve.wait_ge(bad_mm, 1)
                dve.tensor_copy(flag[:, :], ps[:, 4, 0:1]).then_inc(flag_ready, 1)

            def build_group(g, last):
                build_count.start(1 + g * BUILD, 0, BUILD - 1) if last else build_count.start(1, g, BUILD)
                for k in range(UT):
                    if not (last and k == UT - 1):
                        cut_diagonal(g * UT + (k + 1), (k + 1) % 2)
                    code_keys(g * UT + k, k, k % 2)
                    if k == UT - 2:
                        take_products(0, g)
                build_lists(g)

            def elu_input(l, g):
                dve.tensor_scalar(eb, group_of(hid, g), 0.0, None, ALU.min).then_inc(elu_in, 1)

            def normed(g, plink):
                r = group_of(res, g)
                bc = [P, UT, C]
                settled()
                plink(dve.tensor_reduce(mean, r, AX, ALU.add))
                plink(dve.tensor_scalar(mean, mean, -1.0 / C, None, ALU.mult))
                plink(dve.tensor_tensor(r, r, mean.unsqueeze(2).to_broadcast(bc), ALU.add))
                plink(dve.tensor_tensor(sq, r, r, ALU.mult))
                plink(dve.tensor_reduce(var, sq, AX, ALU.add))
                plink(dve.tensor_scalar(var, var, 1.0 / C, EPS, ALU.mult, ALU.add))
                plink(dve.tensor_scalar(yi, var.bitcast(I32), 1, None, ALU.logical_shift_right))
                plink(dve.tensor_scalar(yr.bitcast(I32), yi, -1.0, float(0x5F3759DF), ALU.mult, ALU.add))
                for _ in range(3):
                    plink(dve.tensor_tensor(yt, yr, yr, ALU.mult))
                    plink(dve.scalar_tensor_tensor(out=yt, in0=yt, scalar=-0.5, in1=var, op0=ALU.mult, op1=ALU.mult))
                    plink(dve.scalar_tensor_tensor(out=yr, in0=yt, scalar=1.5, in1=yr, op0=ALU.add, op1=ALU.mult))
                dve.tensor_tensor(group_of(x, g), r, yr.unsqueeze(2).to_broadcast(bc), ALU.mult).then_inc(nodes_ready, 1)

            LN_LINKS = 8 + 9
            POST = {0: 2, 1: 2, 2: 1 + LN_LINKS, 3: 1 + LN_LINKS, 4: 2 + LN_LINKS}

            def post_base(l):
                return sum(POST[k] for k in range(l)) * NGR

            def post_first(l, g, between=None):
                post_count.start(post_base(l), g, POST[l])
                plink = lambda ins: link(ins, post_count, between)
                h = group_of(hid, g)
                if l in ELUS:
                    dve.wait_ge(elu_exp, elu_no(l, g) + 1)
                    plink(dve.scalar_tensor_tensor(out=h, in0=h, scalar=0.0, in1=eb, op0=ALU.max, op1=ALU.add))
                if l < 2:
                    plink(dve.tensor_scalar(sq, group_of(x, g), L0_MIX, L0_MIX - 1.0, ALU.mult, ALU.add))
                    dve.scalar_tensor_tensor(out=h, in0=h, scalar=1.0 - L0_MIX, in1=sq,
                                             op0=ALU.mult, op1=ALU.add).then_inc(nodes_ready, 1)
                    return
                if l == 4:
                    plink(dve.scalar_tensor_tensor(out=group_of(res, g), in0=h, scalar=-1.0, in1=group_of(res, g),
                                                   op0=ALU.add, op1=ALU.add))
                else:
                    plink(dve.tensor_tensor(group_of(res, g), h, group_of(res, g), ALU.add))
                normed(g, plink)

            def post_second(l, g, between=None):
                if l == 1:
                    second_count.start(0, g, LN_LINKS)
                    take_products(2, g)
                    normed(g, lambda ins: link(ins, second_count, between))

            def sparse(l):
                gat = SLOPE[l] is not None
                gb = gats_before(l) * NGR
                f_of = lambda b: feat[:, b, :, :]

                def rows_free(g):
                    if not (l == 0 and isinstance(g, int) and g < 2):
                        dve.wait_ge(stf_ready, g * 2 + (l * NGR - 1) * 2)

                def row_of_edges(g, b, e):
                    o = dve.tensor_scalar(st[:, b, e, :], iotab, rowi[:, bass.ds(g * UT + e // CH, 1), e % CH], None, ALU.is_equal)
                    if e == UT * CH - 1:
                        o.then_inc(st_ready, 1)

                def places(g):
                    if gat:
                        all3 = [P, NE, SLOTS]
                        if not (isinstance(g, int) and g + gb == 0):
                            dve.wait_ge(q_ready, g + gb)
                        dve.tensor_tensor(q, iota[:, 0:SLOTS].unsqueeze(1).to_broadcast(all3),
                                          slot[:, bass.ds(g * NE, NE)].unsqueeze(2).to_broadcast(all3),
                                          ALU.is_equal).then_inc(q_made, 1)

                def edge_scores(g, i, b):
                    dve.wait_ge(q_made, g + (gb + 1))
                    dve.wait_ge(gathered[b], i * (16 * NE) + (l * (NGR // 2) + 1) * 16 * NE)
                    all4 = [P, NE, SLOTS, 3]
                    dve.tensor_tensor(qv, q.unsqueeze(3).to_broadcast(all4),
                                      f_of(b)[:, :, C + 2:C + 5].unsqueeze(2).to_broadcast(all4),
                                      ALU.mult).then_inc(q_ready, 1)

                def parts(o, a, between=None):
                    slink(dve.tensor_copy(o[:, :, 0], a), between)
                    slink(dve.tensor_tensor(mtmp3, a, o[:, :, 0], ALU.subtract), between)
                    slink(dve.tensor_copy(o[:, :, 1], mtmp3), between)
                    return dve.tensor_tensor(o[:, :, 2], mtmp3, o[:, :, 1], ALU.subtract)

                def row_max(g, between):
                    n = bass.ds(g * UT, UT)
                    vown, u = tab[:, n, C], own[:, n]
                    dve.tensor_tensor(vself, vown, dgb[:, n], ALU.add)
                    parts(um[:, :, 0, :], u, between)
                    dve.wait_ge(vp_mm, g + (gb + 1))
                    slink(dve.tensor_reduce(vs, ps[:, 4, 0:UT * SLOTS * 3].rearrange("p (j r) -> p j r", r=3), AX, ALU.add))
                    vs3 = vs.rearrange("p (k s) -> p k s", k=UT)
                    slink(dve.tensor_tensor(vs3, vs3, vbias[:, n, :], ALU.add))
                    slink(dve.tensor_reduce(vmax, vs3, AX, ALU.max))
                    slink(dve.tensor_tensor(vmax, vmax, vself, ALU.max))
                    slink(dve.tensor_tensor(zr, u, vmax, ALU.add))
                    slink(dve.scalar_tensor_tensor(out=mrow, in0=zr, scalar=SLOPE[l], in1=zr, op0=ALU.mult, op1=ALU.max))
                    parts(um[:, :, 1, :], mrow).then_inc(um_ready, 1)

                def self_scores(g):
                    n = bass.ds(g * UT, UT)
                    slink(dve.tensor_tensor(zs, own[:, n], tab[:, n, C], ALU.add))
                    slink(dve.scalar_tensor_tensor(out=zs, in0=zs, scalar=SLOPE[l], in1=zs, op0=ALU.mult, op1=ALU.max))
                    slink(dve.tensor_tensor(zs, zs, mrow, ALU.subtract))
                    dve.tensor_scalar(ws, zs, 0.0, None, ALU.min).then_inc(self_in, 1)

                def edge_inputs(g, b):
                    ue = ps[:, 5, 0:2 * NE * 3].rearrange("p (e a r) -> p e a r", a=2, r=3)
                    dve.wait_ge(um_mm, g + (gb + 1))
                    slink(dve.tensor_reduce(ues, ue, AX, ALU.add))
                    slink(dve.tensor_tensor(we, ues[:, :, 0], f_of(b)[:, :, C], ALU.add))
                    slink(dve.scalar_tensor_tensor(out=we, in0=we, scalar=SLOPE[l], in1=we, op0=ALU.mult, op1=ALU.max))
                    slink(dve.tensor_tensor(we, we, ues[:, :, 1], ALU.subtract))
                    dve.tensor_scalar(we, we, 0.0, None, ALU.min).then_inc(edge_in, 1)

                def scaled(g, b):
                    n = bass.ds(g * UT, UT)
                    dve.wait_ge(edge_exp, g + (gb + 1))
                    dve.tensor_tensor(fs, f_of(b)[:, :, 0:TC], we.unsqueeze(2).to_broadcast([P, NE, TC]),
                                      ALU.mult).then_inc(fs_ready, 1)
                    dve.wait_ge(self_exp, g + (gb + 1))
                    slink(dve.tensor_tensor(ws, ws, dg[:, n], ALU.mult))

                def summed(g):
                    epi_count.start(l * NGR * 3 + sum(k < l for k in ELUS) * NGR, g, 3 + (l in ELUS))
                    n = bass.ds(g * UT, UT)
                    wself = ws if gat else dg[:, n]
                    dve.tensor_tensor(part, tab[:, n, 0:C], wself.unsqueeze(2).to_broadcast([P, UT, C]), ALU.mult)
                    dve.wait_ge(sum_mm, g + (l * NGR + 1))
                    sums = ps[:, 6, 0:UT * TC].rearrange("p (k c) -> p k c", k=UT)
                    elink(dve.tensor_tensor(rd, sums[:, :, C + 1], wself, ALU.add))
                    elink(dve.reciprocal(rd, rd))
                    elink(dve.tensor_tensor(part, part, sums[:, :, 0:C], ALU.add))
                    o = dve.tensor_tensor(group_of(hid, g), part, rd.unsqueeze(2).to_broadcast([P, UT, C]), ALU.mult)
                    if l in ELUS:
                        elink(o)
                        elu_input(l, g)
                    else:
                        o.then_inc(sum_used, 1)
                        dve.wait_ge(sum_used, sum_base + g + 1)

                sum_base = sum(k < l for k in range(NL) if k not in ELUS) * NGR

                def turn_of(g, i, b):
                    if has(g + 1):
                        rows_free(g + 1)
                    chunks = iter(range(UT * CH) if has(g + 1) else ())

                    def between():
                        for e in chunks:
                            row_of_edges(g + 1, 1 - b, e)
                            return
                    Between.fill = between if l == 1 else None
                    if gat and has(g):
                        sparse_count.start(gats_before(l) * NGR * 20, g, 20)
                        edge_scores(g, i, b)
                    if has(g - 1):
                        summed(g - 1)
                    if gat and has(g):
                        row_max(g, between)
                        self_scores(g)
                        edge_inputs(g, b)
                        scaled(g, b)
                    if has(g + 1):
                        places(g + 1)
                    if l < NL - 1 and has(g - VEC_LAG[l]):
                        take_products(AFTER[l][-1], g - VEC_LAG[l], True, between)
                    if has(g - 2):
                        post_second(l, g - 2, between)
                    if has(g - 1):
                        post_first(l, g - 1, between)
                    for e in chunks:
                        row_of_edges(g + 1, 1 - b, e)

                rows_free(0)
                places(0)
                for e in range(UT * CH):
                    row_of_edges(0, 0, e)
                pipelined(dve, turn_of, VEC_LAG[l])

            dve.wait_ge(x_loaded, 16)
            dve.wait_ge(sparse_const, SPARSE_CONSTS)
            first = posc[:, UT * FULL:UT * FULL + 1]
            dve.tensor_scalar(whose[:, 0:1], first, float(CAP), None, ALU.is_lt)
            dve.tensor_scalar(whose[:, 1:2], first, float(CAP), None, ALU.is_ge).then_inc(whose_made, 1)
            dve.wait_ge(whose_made, 1)
            for c in range(UT * FULL, NE):
                o = dve.scalar_tensor_tensor(out=posc[:, c:c + 1], in0=whose[:, 1:2], scalar=-float(P // 2), in1=posc[:, c:c + 1],
                                             op0=ALU.mult, op1=ALU.add)
            o.then_inc(whose_made, 1)
            dve.wait_ge(whose_made, 2)
            build_count.start(0, 0, 1)
            cut_diagonal(0, 0)
            build_group(0, False)
            with dve.Fori(1, NGR - 1) as g:
                build_group(g, False)
            build_group(NGR - 1, True)
            judged()
            dve.wait_ge(flag_ready, 1)
            dense = dve.value_load(flag[0:1, 0:1])
            for l in range(NL):
                with dve.If(dense):
                    if l == 0:
                        for b in range(2):
                            dve.wait_ge(gathered[b], 16 * NE)
                    aggregate(l)
                    with dve.Fori(0, NGR) as g:
                        if l in ELUS:
                            elu_input(l, g)
                        post_first(l, g)
                        post_second(l, g)
                        if l < NL - 1:
                            take_products(AFTER[l][-1], g)
                with dve.Else():
                    sparse(l)


def packed(i):
    f = {k: np.asarray(v) for k, v in i.items()}
    blob = np.zeros((C + 1, BLOB), np.float32)
    tables = [f["L0_gnn_W"][0], f["L0_gnn_W"][1], f["L1_gnn_weight"][:C], f["L2_gnn_weight_w"], f["L3_gnn_W"]]
    rest = [f["L0_gnn_mlp_w"][:C], f["L0_gnn_mlp_w"][C:2 * C], f["L1_gnn_weight"][C:], None, None]
    bias = [f["L0_gnn_mlp_b"], None, f["L1_gnn_bias"], f["L2_gnn_bias"], None]
    for l in range(NL):
        blob[:C, l * RC:l * RC + C] = tables[l]
        if rest[l] is not None:
            blob[:C, l * RC + TC:(l + 1) * RC] = rest[l]
        if bias[l] is not None:
            blob[C, l * RC + TC:(l + 1) * RC] = bias[l]
        if l in WT_OF:
            blob[:C, WT + WT_OF[l] * (C + 1):WT + WT_OF[l] * (C + 1) + C] = tables[l].T
    blob[:C, MLP2:MLP2 + C] = f["L0_gnn_mlp_w"][2 * C:]
    for k, a in enumerate((f["L2_gnn_weight_a"], f["L3_gnn_a"])):
        blob[:C, A2 + 2 * k] = a[C:, 0]
        blob[:C, A2 + 2 * k + 1] = a[:C, 0]
    for l in range(2):
        blob[:HID, LT + 2 * l * C:LT + (2 * l + 1) * C] = f["L0_gnn_lin_w"][l, C:].T
        blob[:HID, LT + (2 * l + 1) * C:LT + (2 * l + 2) * C] = f["L0_gnn_lin_w"][l, :C].T
        blob[:HID, AV + l] = f["L0_gnn_attn"][l, :, 0]
        blob[:HID, LB + l * (C + 1) + C] = f["L0_gnn_lin_b"][l]
    return blob


def kernel(x, adj, **weights):
    import concourse.bacc as bacc
    from concourse.bass_utils import run_bass_kernel_spmd

    arrays = {
        "x": np.ascontiguousarray(x),
        "adj": np.ascontiguousarray(adj),
        "weights": packed(weights),
    }
    nc = bacc.Bacc("TRN2", target_bir_lowering=False, num_devices=1)
    args = [nc.dram_tensor(n, a.shape, mybir.dt.from_np(a.dtype), kind="ExternalInput").ap() for n, a in arrays.items()]
    out = nc.dram_tensor("result", (N, C), F32, kind="ExternalOutput").ap()
    build(nc, *args, out)
    return run_bass_kernel_spmd(nc, [arrays], core_ids=[0]).results[0]["result"]
```
